# Optimizing a Trainium2 kernel written in Bass

```python
import numpy as np
import jax
import jax.numpy as jnp

def _softmax(x, axis=-1):
    return jax.nn.softmax(x, axis=axis)

def _gelu(x):
    return jax.nn.gelu(x, approximate=True)

def _silu(x):
    return jax.nn.silu(x)

def _sigmoid(x):
    return jax.nn.sigmoid(x)

def _layernorm(x, axis=-1, eps=1e-05):
    m = jnp.mean(x, axis=axis, keepdims=True)
    v = jnp.var(x, axis=axis, keepdims=True)
    return (x - m) / jnp.sqrt(v + eps)

def _scatter_add(tgt, idx, src, axis=0):
    return tgt.at[idx].add(src)

def _segment_sum(src, seg, n):
    return jax.ops.segment_sum(src, seg, n)
kernel_name = 'mk_decoder_postln_d1_seqx_r4_07073d'

def setup_inputs(seed: int=0):
    np.random.seed(seed)
    _w = jnp.asarray

    def _rec_inputs():
        import jax
        import jax.numpy as jnp
        _rk = jax.random.key(seed)
        x = -7.109e-05 + 0.9999 * jax.random.normal(jax.random.fold_in(_rk, 1), (8, 256, 1024), jnp.float32)
        _lenS = 256 - jax.random.randint(jax.random.fold_in(_rk, 7), (8,), 0, max(1, 256 // 4) + 1, jnp.int32)
        _lenS2 = 256 - jax.random.randint(jax.random.fold_in(_rk, 8), (8,), 0, max(1, 256 // 4) + 1, jnp.int32)
        _ctx_4096P = jax.random.normal(jax.random.fold_in(_rk, 11), (8, 16, 1024), jnp.float32)
        _ctx_4096c = jax.random.dirichlet(jax.random.fold_in(_rk, 511), 0.3 * jnp.ones((16,), jnp.float32), (8, 256))
        _ctx_4096t = jnp.einsum('bsk,bkd->bsd', _ctx_4096c, _ctx_4096P)
        _ctx_4096t = _ctx_4096t * jax.lax.rsqrt(jnp.mean(jnp.square(_ctx_4096t)) + 1e-12) * 0.953939
        ctx_4096 = -2.6191e-05 + 0.999952 * (_ctx_4096t + 0.3 * jax.random.normal(jax.random.fold_in(_rk, 611), (8, 256, 1024), jnp.float32))
        return (x, ctx_4096)
    x, ctx_4096 = _rec_inputs()

    def _L0_attn_setup():
        import jax, jax.numpy as jnp
        import numpy as np
        N_HEADS = 32
        N_KV_HEADS = 8
        DIM = 1024
        HEAD_DIM = DIM // N_HEADS
        N_REP = N_HEADS // N_KV_HEADS
        ROPE_THETA = 10000.0

        def _apply_rope(x):
            seq = x.shape[2]
            hd = x.shape[-1]
            inv_freq = 1.0 / ROPE_THETA ** (jnp.arange(0, hd, 2, dtype=jnp.float32) / hd)
            angles = jnp.arange(seq, dtype=jnp.float32)[:, None] * inv_freq[None, :]
            cos = jnp.cos(angles)[None, None]
            sin = jnp.sin(angles)[None, None]
            x1 = x[..., 0::2]
            x2 = x[..., 1::2]
            r1 = x1 * cos - x2 * sin
            r2 = x1 * sin + x2 * cos
            return jnp.stack([r1, r2], axis=-1).reshape(x.shape)
        key = jax.random.key(seed)
        k1, k2, k3 = jax.random.split(key, 3)
        bs, seq = (1, 512)
        x = jax.random.normal(k1, (bs, seq, DIM), dtype=jnp.float32)
        w_qkv = jax.random.normal(k2, (DIM, HEAD_DIM * (N_HEADS + 2 * N_KV_HEADS)), dtype=jnp.float32) * 0.02
        w_o = jax.random.normal(k3, (N_HEADS * HEAD_DIM, DIM), dtype=jnp.float32) * 0.02
        return {'x': x, 'w_qkv': w_qkv, 'w_o': w_o}
    _L0_attn_all = _L0_attn_setup()
    _L0_attn_in = {k: v for k, v in _L0_attn_all.items() if k in ('w_qkv', 'w_o')}
    del _L0_attn_all

    def _L0_xattn_setup():
        import jax, jax.numpy as jnp
        import numpy as np
        TEXT_DIM = 1024
        FEATURE_DIM = 1024

        def _xavier_uniform(key, shape):
            fan_in, fan_out = (shape[1], shape[0])
            limit = float(np.sqrt(6.0 / (fan_in + fan_out)))
            return jax.random.uniform(key, shape, jnp.float32, -limit, limit)
        key = jax.random.key(seed)
        k1, k2, k3, k4 = jax.random.split(key, 4)
        text = jax.random.normal(k1, (8, 512, TEXT_DIM), jnp.float32)
        features = jax.random.normal(k2, (8, 144, FEATURE_DIM), jnp.float32)
        Wq = _xavier_uniform(k3, (FEATURE_DIM, TEXT_DIM))
        bq = jnp.zeros((FEATURE_DIM,), jnp.float32)
        Wk = _xavier_uniform(k4, (FEATURE_DIM, FEATURE_DIM))
        bk = jnp.zeros((FEATURE_DIM,), jnp.float32)
        return {'text': text, 'features': features, 'Wq': Wq, 'bq': bq, 'Wk': Wk, 'bk': bk}
    _L0_xattn_all = _L0_xattn_setup()
    _L0_xattn_in = {k: v for k, v in _L0_xattn_all.items() if k in ('Wq', 'bq', 'Wk', 'bk')}
    del _L0_xattn_all

    def _L0_ffn_setup():
        import jax, jax.numpy as jnp
        import numpy as np
        B_L, B_H = (4, 8)
        LIN_SLOPE, LIN_INTER, EST_T = (1.0, 0.0, 64.0)
        BATCH, SEQ, IN_F, OUT_F = (4, 512, 1024, 1024)
        MAX_BITS = 8

        def dequant_kbit(qweight, lut, bit):
            O, I32 = (qweight.shape[1], qweight.shape[2])
            shifts = jnp.arange(32, dtype=jnp.int32)
            idx = jnp.zeros((O, I32 * 32), dtype=jnp.int32)
            for p in range(bit):
                bits = (qweight[p][:, :, None] >> shifts & 1).reshape(O, I32 * 32)
                idx = idx | bits << p
            return jnp.take_along_axis(lut, idx, axis=1)
        key = jax.random.key(seed)
        k = jax.random.split(key, 5)
        x = jax.random.normal(k[0], (BATCH, SEQ, IN_F), dtype=jnp.float32)
        qweight = jax.random.randint(k[1], (MAX_BITS, OUT_F, IN_F // 32), 0, 2147483647, dtype=jnp.int32)
        lut4 = jax.random.normal(k[2], (OUT_F, 2 ** B_L), dtype=jnp.float32) * 0.02
        lut8 = jax.random.normal(k[3], (OUT_F, 2 ** B_H), dtype=jnp.float32) * 0.02
        bias = jax.random.normal(k[4], (OUT_F,), dtype=jnp.float32) * 0.01
        return {'x': x, 'qweight': qweight, 'lut4': lut4, 'lut8': lut8, 'bias': bias}
    _L0_ffn_all = _L0_ffn_setup()
    _L0_ffn_in = {k: v for k, v in _L0_ffn_all.items() if k in ('qweight', 'lut4', 'lut8', 'bias')}
    del _L0_ffn_all
    return {'x': x, 'ctx_4096': ctx_4096, 'L0_attn_w_qkv': _L0_attn_in['w_qkv'], 'L0_attn_w_o': _L0_attn_in['w_o'], 'L0_xattn_Wq': _L0_xattn_in['Wq'], 'L0_xattn_bq': _L0_xattn_in['bq'], 'L0_xattn_Wk': _L0_xattn_in['Wk'], 'L0_xattn_bk': _L0_xattn_in['bk'], 'L0_ffn_qweight': _L0_ffn_in['qweight'], 'L0_ffn_lut4': _L0_ffn_in['lut4'], 'L0_ffn_lut8': _L0_ffn_in['lut8'], 'L0_ffn_bias': _L0_ffn_in['bias']}

def reference(x, ctx_4096, L0_attn_w_qkv, L0_attn_w_o, L0_xattn_Wq, L0_xattn_bq, L0_xattn_Wk, L0_xattn_bk, L0_ffn_qweight, L0_ffn_lut4, L0_ffn_lut8, L0_ffn_bias):
    import jax
    import jax.numpy as jnp

    def _L0_attn_ref(x, w_qkv, w_o):
        import jax, jax.numpy as jnp
        import numpy as np
        N_HEADS = 32
        N_KV_HEADS = 8
        DIM = 1024
        HEAD_DIM = DIM // N_HEADS
        N_REP = N_HEADS // N_KV_HEADS
        ROPE_THETA = 10000.0

        def _apply_rope(x):
            seq = x.shape[2]
            hd = x.shape[-1]
            inv_freq = 1.0 / ROPE_THETA ** (jnp.arange(0, hd, 2, dtype=jnp.float32) / hd)
            angles = jnp.arange(seq, dtype=jnp.float32)[:, None] * inv_freq[None, :]
            cos = jnp.cos(angles)[None, None]
            sin = jnp.sin(angles)[None, None]
            x1 = x[..., 0::2]
            x2 = x[..., 1::2]
            r1 = x1 * cos - x2 * sin
            r2 = x1 * sin + x2 * cos
            return jnp.stack([r1, r2], axis=-1).reshape(x.shape)
        bs, seq, _ = x.shape
        qkv = x @ w_qkv
        q_sz = N_HEADS * HEAD_DIM
        kv_sz = N_KV_HEADS * HEAD_DIM
        xq = qkv[..., :q_sz].reshape(bs, seq, N_HEADS, HEAD_DIM).transpose(0, 2, 1, 3)
        xk = qkv[..., q_sz:q_sz + kv_sz].reshape(bs, seq, N_KV_HEADS, HEAD_DIM).transpose(0, 2, 1, 3)
        xv = qkv[..., q_sz + kv_sz:].reshape(bs, seq, N_KV_HEADS, HEAD_DIM).transpose(0, 2, 1, 3)
        xq = _apply_rope(xq)
        xk = _apply_rope(xk)
        keys = jnp.repeat(xk, N_REP, axis=1)
        values = jnp.repeat(xv, N_REP, axis=1)
        scale = 1.0 / jnp.sqrt(jnp.float32(HEAD_DIM))
        scores = jnp.einsum('bhsd,bhtd->bhst', xq, keys) * scale
        causal = jnp.tril(jnp.ones((seq, seq), dtype=bool))[None, None]
        scores = jnp.where(causal, scores, -jnp.inf)
        probs = jax.nn.softmax(scores, axis=-1)
        out = jnp.einsum('bhst,bhtd->bhsd', probs, values)
        out = out.transpose(0, 2, 1, 3).reshape(bs, seq, N_HEADS * HEAD_DIM)
        return out @ w_o

    def _L0_xattn_ref(text, features, Wq, bq, Wk, bk):
        import jax, jax.numpy as jnp
        import numpy as np
        TEXT_DIM = 1024
        FEATURE_DIM = 1024

        def _xavier_uniform(key, shape):
            fan_in, fan_out = (shape[1], shape[0])
            limit = float(np.sqrt(6.0 / (fan_in + fan_out)))
            return jax.random.uniform(key, shape, jnp.float32, -limit, limit)
        Q = jnp.einsum('btx,dx->btd', text, Wq) + bq
        K = jnp.einsum('bpx,dx->bpd', features, Wk) + bk
        scale = 1.0 / jnp.sqrt(jnp.asarray(K.shape[-1], K.dtype))
        scores = jnp.einsum('btd,bpd->btp', Q, K) * scale
        attn = jax.nn.softmax(scores, axis=-1)
        attended = jnp.einsum('btp,bpd->btd', attn, features)
        return attended

    def _L0_ffn_ref(x, qweight, lut4, lut8, bias):
        import jax, jax.numpy as jnp
        import numpy as np
        B_L, B_H = (4, 8)
        LIN_SLOPE, LIN_INTER, EST_T = (1.0, 0.0, 64.0)
        BATCH, SEQ, IN_F, OUT_F = (4, 512, 1024, 1024)
        MAX_BITS = 8

        def dequant_kbit(qweight, lut, bit):
            O, I32 = (qweight.shape[1], qweight.shape[2])
            shifts = jnp.arange(32, dtype=jnp.int32)
            idx = jnp.zeros((O, I32 * 32), dtype=jnp.int32)
            for p in range(bit):
                bits = (qweight[p][:, :, None] >> shifts & 1).reshape(O, I32 * 32)
                idx = idx | bits << p
            return jnp.take_along_axis(lut, idx, axis=1)
        e = jnp.linalg.norm(x, axis=-1) * LIN_SLOPE + LIN_INTER
        mask = e > EST_T
        w_l = dequant_kbit(qweight, lut4, B_L)
        w_h = dequant_kbit(qweight, lut8, B_H)
        y_l = jnp.einsum('bsi,oi->bso', x, w_l)
        y_h = jnp.einsum('bsi,oi->bso', x, w_h)
        y = jnp.where(mask[..., None], y_h, y_l) + bias
        return y
    x = _layernorm(x + _L0_attn_ref(x, L0_attn_w_qkv, L0_attn_w_o), axis=-1)
    x = _layernorm(x + _L0_xattn_ref(x, ctx_4096, L0_xattn_Wq, L0_xattn_bq, L0_xattn_Wk, L0_xattn_bk), axis=-1)
    x = _layernorm(x + _L0_ffn_ref(x, L0_ffn_qweight, L0_ffn_lut4, L0_ffn_lut8, L0_ffn_bias), axis=-1)
    return x

_drawn_inputs = setup_inputs


def setup_inputs(seed=0):
    import zlib

    import numpy as np

    out = dict(_drawn_inputs(seed))
    spreads = {'L0_xattn_bq': (0.0, 0.431), 'L0_xattn_bk': (0.0, 0.8)}
    factors = {'L0_ffn_bias': 6.777}
    for name, (base, spread) in spreads.items():
        noise = np.random.default_rng([zlib.crc32(name.encode()), seed]).standard_normal(out[name].shape)
        drawn = base * np.exp(spread * noise) if base else spread * noise
        out[name] = jnp.asarray(drawn.astype(out[name].dtype))
    for name, factor in factors.items():
        out[name] = (out[name] * factor).astype(out[name].dtype)
    return out
```

```python
import math
from contextlib import ExitStack

import numpy as np

import concourse.bass as bass
from concourse import mybir

F32, F32R, I32 = mybir.dt.float32, mybir.dt.float32r, mybir.dt.int32
ALU, ACT, AX = mybir.AluOpType, mybir.ActivationFunctionType, mybir.AxisListType

P = 128
BATCH, SEQ, D = 8, 256, 1024
TOK = BATCH * SEQ
TILES = TOK // P
KT = D // P
HEADS, KVH, HD = 32, 8, 32
REP = HEADS // KVH
KCOLS = KVH * HD
QKV = HEADS * HD + 2 * KCOLS
ROPE = HEADS * HD + KCOLS
RB = ROPE // P
BANK = 512
CHUNKS = KVH // 2
EPS = 1e-5
MASKED = -1e30
BITS, LEVELS = 4, 16
GROUP = 512
GT = GROUP // P
GROUPS = TOK // GROUP
CROSS_SCALE = 1.0 / math.sqrt(D)


def rope_tables():
    inv = (np.float32(1.0) / np.float32(10000.0) ** (np.arange(0, HD, 2, dtype=np.float32) / np.float32(HD)))
    ang = np.arange(SEQ, dtype=np.float32)[:, None] * inv.astype(np.float32)[None, :]
    c, s = np.cos(ang).astype(np.float32), np.sin(ang).astype(np.float32)
    one = np.concatenate([np.repeat(c, 2, axis=1), -s, s], axis=1)
    return np.ascontiguousarray(np.stack([one, one * np.float32(1.0 / math.sqrt(HD))], axis=1).astype(np.float32))


def decoder_layer(nc, x, ctx_in, w_qkv, w_o, wq, bq, wk, bk, qweight, lut4, bias, rope, out):
    qk_scr = nc.dram_tensor("qk_scr", (2, ROPE, TOK), F32, kind="Internal").ap()
    v_scr = nc.dram_tensor("v_scr", (TOK, KCOLS), F32, kind="Internal").ap()
    x1_scr = nc.dram_tensor("x1_scr", (TOK, D), F32, kind="Internal").ap()
    x2_scr = nc.dram_tensor("x2_scr", (TOK, D), F32, kind="Internal").ap()
    wl_scr = nc.dram_tensor("wl_scr", (D, D), F32, kind="Internal").ap()

    xt, cx = x.rearrange("b s d -> (b s) d"), ctx_in.rearrange("b s d -> (b s) d")
    ot = out.rearrange("b s d -> (b s) d")

    top = ExitStack()
    with top:
        def area():
            stack = ExitStack()

            def sb(name, shape, dt=F32):
                return stack.enter_context(nc.sbuf_tensor(name, shape, dt))
            return stack, sb

        def sem(name):
            return top.enter_context(nc.semaphore(name))

        def sems(name, n):
            return [sem(f"{name}{i}") for i in range(n)]

        bank = [top.enter_context(nc.psum_tensor(f"bank{i}", [P, BANK], F32)) for i in range(8)]

        def const(name, shape, dt=F32):
            return top.enter_context(nc.sbuf_tensor(name, shape, dt))

        ident = const("ident", [P, P])
        ident_r = const("ident_r", [P, P], F32R)
        mask_r = const("mask_r", [P, REP, P], F32R)
        ones_r = const("ones_r", [P, P], F32R)
        neg_half = const("neg_half", [P, 1])
        tab = const("tab", [P, 2, 2, 2 * HD])

        a1, sb = area()
        w_hi, w_lo = sb("w_hi", [P, KT, QKV], F32R), sb("w_lo", [P, KT, QKV], F32R)
        xT_hi, xT_lo = sb("xT_hi", [P, 2, KT, P], F32R), sb("xT_lo", [P, 2, KT, P], F32R)
        qT_hi, qT_lo = sb("qT_hi", [P, RB, P], F32R), sb("qT_lo", [P, RB, P], F32R)
        x_st = sb("x_st", [P, 2, D])
        w_st = sb("w_st", [P, 2, QKV])
        raw = sb("raw", [P, ROPE])
        rot_c, rot_s, turned = sb("rot_c", [P, ROPE]), sb("rot_s", [P, ROPE]), sb("turned", [P, ROPE])
        v_st = sb("v_st", [P, 2, KCOLS])
        planes = sb("planes", [P, BITS, D // 32], I32)
        lut = sb("lut", [P, LEVELS])
        lut_x = sb("lut_x", [P, LEVELS // 2], I32)
        bits = sb("bits", [P, BITS, D], I32)
        pick = [sb(f"pick{i}", [P, D], I32) for i in range(4)]
        a1.close()

        a2, sb = area()
        wo_hi, wo_lo = sb("wo_hi", [P, KT, D], F32R), sb("wo_lo", [P, KT, D], F32R)
        q3 = sb("q3", [96, CHUNKS, 2 * REP, SEQ], F32R)
        k3 = sb("k3", [96, CHUNKS, 2, SEQ], F32R)
        vch = sb("vch", [P, CHUNKS, 2, 2 * HD])
        prob = sb("prob", [P, 4, BANK])
        probT = sb("probT", [P, 3, BANK])
        nmax, rsum, rinv = sb("nmax", [P, 4, REP]), sb("rsum", [P, 4, REP]), sb("rinv", [P, 4, REP])
        att = sb("att", [P, KT, SEQ])
        att_hi, att_lo = sb("att_hi", [P, KT, SEQ], F32R), sb("att_lo", [P, KT, SEQ], F32R)
        xr = sb("xr", [P, 2, D])
        y1 = sb("y1", [P, 2, D])
        wo_st = sb("wo_st", [P, 2, D])
        st1, mv1, rs1 = sb("st1", [P, 2, 2, 6]), sb("mv1", [P, 2, 2]), sb("rs1", [P, 2, 2])
        a2.close()

        a4, sb = area()
        m_hi, m_lo = sb("m_hi", [P, KT, D], F32R), sb("m_lo", [P, KT, D], F32R)
        bA, cD = sb("bA", [P, KT]), sb("cD", [P, 1])
        u_pad = sb("u_pad", [P, KT, P], F32R)
        ctx_st = sb("ctx_st", [P, 2, GT, D])
        x1_st = sb("x1_st", [P, GT, D])
        a3 = ExitStack()

        def sb3(name, shape, dt=F32):
            return a3.enter_context(nc.sbuf_tensor(name, shape, dt))
        wq_hi, wq_lo = sb3("wq_hi", [P, KT, D], F32R), sb3("wq_lo", [P, KT, D], F32R)
        wk_hi, wk_lo = sb3("wk_hi", [P, 2, KT, P], F32R), sb3("wk_lo", [P, 2, KT, P], F32R)
        wq_st = x1_st[:, 2:4, :]
        wk_st = ctx_st[:, 1, 0:2, :].rearrange("p s (t c) -> p s t c", c=P)
        b_raw = sb3("b_raw", [P, 2, KT])
        b_hl = sb3("b_hl", [P, 2, KT, 2], F32R)
        b_prod, b_part = sb3("b_prod", [P, KT]), sb3("b_part", [P, 1])
        sel0 = sb3("sel0", [P, P])
        u_col = sb3("u_col", [P, KT])
        a3.close()
        cT_hi, cT_lo = sb("cT_hi", [P, KT, GROUP], F32R), sb("cT_lo", [P, KT, GROUP], F32R)
        k_hi, k_lo = sb("k_hi", [P, KT, GROUP], F32R), sb("k_lo", [P, KT, GROUP], F32R)
        x1T_hi, x1T_lo = sb("x1T_hi", [P, KT, P], F32R), sb("x1T_lo", [P, KT, P], F32R)
        d_hi, d_lo = sb("d_hi", [P, GROUP], F32R), sb("d_lo", [P, GROUP], F32R)
        pc, pcT = sb("pc", [P, 2, SEQ]), sb("pcT", [P, 2, 2, P])
        nm2, rs2, ri2 = sb("nm2", [P, GT, 2]), sb("rs2", [P, GT]), sb("ri2", [P, GT])
        st2, mv2, rv2 = sb("st2", [P, GT, 2, 6]), sb("mv2", [P, GT, 2]), sb("rv2", [P, GT, 2])
        a4.close()

        a5, sb = area()
        f_hi, f_lo = sb("f_hi", [P, KT, D], F32R), sb("f_lo", [P, KT, D], F32R)
        sb("over_bA", [P, KT]), sb("over_cD", [P, 1]), sb("over_u", [P, KT, P])
        x2_st = sb("x2_st", [P, 2, D])
        x2b = sb("x2b", [P, 2, D])
        y3 = sb("y3", [P, 2, D])
        x2T_hi, x2T_lo = sb("x2T_hi", [P, 2, KT, P], F32R), sb("x2T_lo", [P, 2, KT, P], F32R)
        bias_bc = sb("bias_bc", [P, D])
        sb("over_rest", [P, 3 * GT * D - 11 * D])
        f_st = sb("f_st", [P, KT, D])
        st3, mv3, rv3 = sb("st3", [P, 2, 2, 6]), sb("mv3", [P, 2, 2]), sb("rv3", [P, 2, 2])
        a5.close()

        consts_done = sem("consts_done")
        consts_step = sem("consts_step")
        tab_ld = sem("tab_ld")
        w_ld, x_ld = sems("w_ld", 2), sems("x_ld", 2)
        w_hi_ready, w_lo_ready = sem("w_hi_ready"), sem("w_lo_ready")
        xps_ready, xT_hi_ready, xT_lo_ready = sem("xps_ready"), sem("xT_hi_ready"), sem("xT_lo_ready")
        qkv_done, raw_ready, cos_done, sin_done, turned_ready = (
            sems("qkv_done", 3), sems("raw_ready", 3), sems("cos_done", 3), sems("sin_done", 3), sems("turned_ready", 3))
        qps_ready, qT_hi_ready, qT_lo_ready = sems("qps_ready", 3), sem("qT_hi_ready"), sem("qT_lo_ready")
        qhi_st, qlo_st, v_stored = sem("qhi_st"), sem("qlo_st"), sems("v_stored", 2)
        code_ld, bits_ready, lutx_ready, pick_step, wl_stored = (
            sem("code_ld"), sem("bits_ready"), sem("lutx_ready"), sem("pick_step"), sem("wl_stored"))
        wo_ld, wo_hi_ready, wo_lo_ready = sems("wo_ld", 2), sem("wo_hi_ready"), sem("wo_lo_ready")
        chunk_ld, s_done, nmax_ready, exp_done, rinv_ready, prob_ready = (
            sems("chunk_ld", CHUNKS), sem("s_done"), sem("nmax_ready"), sem("exp_done"), sem("rinv_ready"), sem("prob_ready"))
        pT_done, pT_act, pT_dve, pv_done, att_ready, att_hi_ready, att_lo_ready = (
            sem("pT_done"), sem("pT_act"), sem("pT_dve"), sem("pv_done"), sem("att_ready"), sem("att_hi_ready"),
            sem("att_lo_ready"))
        wo_done, y1_part, y1_stats, y1_var, y1_rstd, y1_ready, xr_ld, x1_stored, y1_mv = (
            sem("wo_done"), sem("y1_part"), sem("y1_stats"), sem("y1_var"), sem("y1_rstd"), sem("y1_ready"),
            sems("xr_ld", 2), sems("x1_stored", 2), sem("y1_mv"))
        wq_ld, wk_ld, b_ld = sems("wq_ld", 2), sems("wk_ld", 2), sem("b_ld")
        wq_hi_ready, wq_lo_ready, wk_hi_ready, wk_lo_ready = (
            sem("wq_hi_ready"), sem("wq_lo_ready"), sem("wk_hi_ready"), sem("wk_lo_ready"))
        sel0_ready, bhi_ready, blo_ready, bpart_ready, bA_done, bA_ready, cps_done, cD_ready, bprod_ready = (
            sem("sel0_ready"), sem("bhi_ready"), sem("blo_ready"), sem("bpart_ready"), sem("bA_done"), sem("bA_ready"),
            sem("cps_done"), sem("cD_ready"), sem("bprod_ready"))
        m_done, m_hi_ready, m_lo_ready, u_done, ucol_ready, uhi_ready, upad_ready = (
            sem("m_done"), sem("m_hi_ready"), sem("m_lo_ready"), sem("u_done"), sem("ucol_ready"), sem("uhi_ready"),
            sem("upad_ready"))
        ctx_ld, x1_ld = sems("ctx_ld", 2), sems("x1_ld", GT)
        tps_ready, tps_free, cT_hi_ready, x1T_hi_ready = (
            sem("tps_ready"), sem("tps_free"), sem("cT_hi_ready"), sem("x1T_hi_ready"))
        acc_done, acc_free, k_hi_ready, d_done, d_hi_ready, d_lo_ready = (
            sem("acc_done"), sem("acc_free"), sem("k_hi_ready"), sem("d_done"), sem("d_hi_ready"),
            sem("d_lo_ready"))
        s2_done, nmax2_raw, nmax2_ready, exp2_done, rinv2_ready, p2T_done, p2T_ready = (
            sem("s2_done"), sem("nmax2_raw"), sem("nmax2_ready"), sem("exp2_done"), sem("rinv2_ready"), sem("p2T_done"),
            sem("p2T_ready"))
        y2_part, y2_stats, y2_mv, y2_var, y2_rstd, y2_ready, x2_stored = (
            sem("y2_part"), sem("y2_stats"), sem("y2_mv"), sem("y2_var"), sem("y2_rstd"), sem("y2_ready"),
            sems("x2_stored", GT))
        f_ld, fps_done, f_hi_ready, f_lo_ready, bias_ld, x2_ld = (
            sem("f_ld"), sem("fps_done"), sem("f_hi_ready"), sem("f_lo_ready"), sem("bias_ld"), sems("x2_ld", 2))
        x2ps_ready, x2T_hi_ready, x2T_lo_ready, x2b_ready, ffn_done = (
            sem("x2ps_ready"), sem("x2T_hi_ready"), sem("x2T_lo_ready"), sem("x2b_ready"), sem("ffn_done"))
        y3_part, y3_stats, y3_mv, y3_var, y3_rstd, y3_ready, out_stored = (
            sem("y3_part"), sem("y3_stats"), sem("y3_mv"), sem("y3_var"), sem("y3_rstd"), sem("y3_ready"),
            sems("out_stored", 2))

        CHUNK_BANK = (bank[0], bank[1], bank[2])
        XPS = (bank[3], bank[4])
        QPS = (bank[5], bank[6], bank[7])
        QBLK = ((0, 4), (4, 8), (8, 10))
        PIECE = (((0, 256, 0), (256, 512, 1)), ((512, 1024, 1),), ((1024, 1280, 1),))

        PICKS = 15

        SUB = 3 * KVH
        LAG = 3
        SBANK = (bank[0], bank[1], bank[2])
        TBANK = (bank[3], bank[4])
        OBANK = bank[5]
        WBANK = (bank[6], bank[7])
        WO_FIRST, WO_LAST = 5, 22
        SPLIT_STEP = {0: 0, 1: 1, 2: 2, 4: 3}

        def heads_of(pos):
            return (0, 1) if pos == 0 else (2, 3) if pos == 1 else (0, 1, 2, 3)

        def keys_of(pos):
            return 2 * P if pos < 2 else P

        block = top.enter_context(nc.Block())


        def wait(eng, s, value):
            if not (isinstance(value, int) and value <= 0):
                eng.wait_ge(s, value)

        def wait_alone(eng, s, value):
            wait(eng, s, value)
            eng.nop(nofuse=True)

        @block.sync
        def _(sp):
            sp.dma_start(x_st[:, 0, :], xt[0:P, :]).then_inc(x_ld[0], 16)
            for kt in range(KT):
                wait(sp, w_lo_ready, kt - 1)
                sp.dma_start(w_st[:, kt % 2, :], w_qkv[kt * P:(kt + 1) * P, :]).then_inc(w_ld[kt % 2], 16)
                if kt == 1:
                    sp.dma_start(x_st[:, 1, :], xt[P:2 * P, :]).then_inc(x_ld[1], 16)
                    sp.dma_start(tab[:, :, :, :], rope.rearrange("(j p) t c -> p j t c", p=P)).then_inc(tab_ld, 16)
            sp.wait_ge(xps_ready, 2)
            sp.dma_start(x_st[:, 0, :], xt[2 * P:3 * P, :]).then_inc(x_ld[0], 16)

            def load_codes(b):
                sp.dma_start(planes[:, :, :], qweight[0:BITS, bass.ds(b * P, P), :].rearrange("q o w -> o q w"))\
                  .then_inc(code_ld, 16)
                sp.dma_start(lut[:, :], lut4[bass.ds(b * P, P), :]).then_inc(code_ld, 16)

            def stage1_batch(b, ahead, codes):
                for j in range(2):
                    n = 2 * b + j
                    if ahead[j]:
                        sp.wait_ge(xps_ready, 2 * n + 4)
                        sp.dma_start(x_st[:, 1 - j, :], xt[bass.ds((n + 3) * P, P), :]).then_inc(x_ld[1 - j], 16)
                    sp.wait_ge(raw_ready[2], n + 1)
                    sp.dma_start(v_scr[bass.ds(n * P, P), :], v_st[:, j, :]).then_inc(v_stored[j], 16)
                    wait_alone(sp, qT_hi_ready, 3 * n + 3)
                    sp.dma_start(qk_scr[0].rearrange("(c p) s -> p c s", p=P)[:, :, bass.ds(n * P, P)],
                                 qT_hi[:, :, :].bitcast(F32)).then_inc(qhi_st, 16)
                    sp.wait_ge(qT_lo_ready, n + 1)
                    sp.dma_start(qk_scr[1].rearrange("(c p) s -> p c s", p=P)[:, :, bass.ds(n * P, P)],
                                 qT_lo[:, :, :].bitcast(F32)).then_inc(qlo_st, 16)
                sp.wait_ge(pick_step, PICKS * b + PICKS)
                sp.dma_start(wl_scr[bass.ds(b * P, P), :], pick[0][:, :].bitcast(F32)).then_inc(wl_stored, 16)
                if codes:
                    load_codes(b + 1)

            load_codes(0)
            with sp.Fori(0, BATCH - 2) as b:
                stage1_batch(b, (True, True), True)
            stage1_batch(BATCH - 2, (True, False), True)
            stage1_batch(BATCH - 1, (False, False), False)

            sp.wait_ge(qhi_st, 16 * TILES)
            sp.wait_ge(qlo_st, 16 * TILES)
            sp.wait_ge(v_stored[0], 16 * BATCH)
            sp.wait_ge(v_stored[1], 16 * BATCH)
            sp.wait_ge(wl_stored, 16 * BATCH)

            def load_chunk(b, q):
                wait(sp, pv_done, KVH * b + 2 * q + 2 - KVH)
                s = bass.ds(b * SEQ, SEQ)
                for part, (qp, kp) in enumerate(((0, 0), (0, 1), (1, 0))):
                    rows = slice(32 * part, 32 * part + 32)
                    sp.dma_start(q3[rows, q, :, :].bitcast(F32),
                                 qk_scr[qp, KCOLS + 2 * P * q:KCOLS + 2 * P * (q + 1), s].rearrange(
                                     "(h d) s -> d h s", d=HD)).then_inc(chunk_ld[q], 16)
                    sp.dma_start(k3[rows, q, :, :].bitcast(F32),
                                 qk_scr[kp, 2 * HD * q:2 * HD * (q + 1), s].rearrange("(h d) s -> d h s", d=HD))\
                      .then_inc(chunk_ld[q], 16)
                sp.dma_start(vch[:, q, :, :], v_scr[s, 2 * HD * q:2 * HD * (q + 1)].rearrange(
                    "(t p) c -> p t c", p=P)).then_inc(chunk_ld[q], 16)

            def load_wo(kt):
                wait(sp, wo_lo_ready, kt - 1)
                sp.dma_start(wo_st[:, kt % 2, :], w_o[kt * P:(kt + 1) * P, :]).then_inc(wo_ld[kt % 2], 16)

            def load_x(b, st):
                sp.dma_start(xr[:, st, :], xt[bass.ds(b * SEQ + st * P, P), :]).then_inc(xr_ld[st], 16)

            def store_x1(b, st):
                sp.wait_ge(y1_ready, 2 * b + st + 1)
                sp.dma_start(x1_scr[bass.ds(b * SEQ + st * P, P), :], y1[:, st, :]).then_inc(x1_stored[st], 16)

            for q in range(CHUNKS):
                load_chunk(0, q)
            for st in range(2):
                sp.sem_inc(x1_stored[st], 16)
                load_x(0, st)
            for kt in range(KT):
                load_wo(kt)
            for q in range(CHUNKS - 1):
                load_chunk(1, q)

            def stage2_batch(b, last):
                load_chunk(b, CHUNKS - 1)
                if not last:
                    load_chunk(b + 1, 0)
                    load_chunk(b + 1, 1)
                store_x1(b - 1, 0)
                load_x(b, 0)
                if not last:
                    load_chunk(b + 1, 2)
                store_x1(b - 1, 1)
                load_x(b, 1)
            with sp.Fori(1, BATCH - 1) as b:
                stage2_batch(b, False)
            stage2_batch(BATCH - 1, True)
            for st in range(2):
                store_x1(BATCH - 1, st)

            sp.wait_ge(x1_stored[0], 16 * BATCH + 16)
            sp.wait_ge(x1_stored[1], 16 * BATCH + 16)

            def load_wk(m):
                wait(sp, wk_lo_ready, m - 1)
                sp.dma_start(wk_st[:, m % 2, :, :], wk[:, m * P:(m + 1) * P].rearrange("(t p) c -> p t c", p=P))\
                  .then_inc(wk_ld[m % 2], 16)
            for i, v in enumerate((bq, bk)):
                with nc.allow_non_contiguous_dma(reason="two short vectors, once"):
                    sp.dma_start(b_raw[:, i, :], v.rearrange("(t p) -> p t", p=P)).then_inc(b_ld, 16)
            load_wk(0)
            load_wk(1)
            for dt in range(KT):
                wait(sp, wq_lo_ready, dt - 1)
                sp.dma_start(wq_st[:, dt % 2, :], wq[dt * P:(dt + 1) * P, :]).then_inc(wq_ld[dt % 2], 16)

            def load_ctx(g):
                wait(sp, acc_done, 2 * KT * (g - 1))
                for t in range(GT):
                    sp.dma_start(ctx_st[:, g % 2, t, :], cx[g * GROUP + t * P:g * GROUP + (t + 1) * P, :])\
                      .then_inc(ctx_ld[g % 2], 16)

            def load_x1(g, t):
                wait(sp, x2_stored[t], 16 * g)
                sp.dma_start(x1_st[:, t, :], x1_scr[g * GROUP + t * P:g * GROUP + (t + 1) * P, :])\
                  .then_inc(x1_ld[t], 16)

            load_ctx(0)
            sp.wait_ge(wq_lo_ready, KT)
            for t in range(GT):
                load_x1(0, t)
            for m in range(2, KT):
                load_wk(m)
            sp.wait_ge(wk_lo_ready, KT)
            load_ctx(1)
            for g in range(GROUPS):
                for t in range(GT):
                    sp.wait_ge(y2_ready, GT * g + t + 1)
                    sp.dma_start(x2_scr[g * GROUP + t * P:g * GROUP + (t + 1) * P, :], x1_st[:, t, :])\
                      .then_inc(x2_stored[t], 16)
                if g + 2 < GROUPS:
                    load_ctx(g + 2)
                if g + 1 < GROUPS:
                    for t in range(GT):
                        load_x1(g + 1, t)
                if g == GROUPS - 2:
                    sp.wait_ge(d_done, GROUPS)
                    for o in range(KT):
                        sp.dma_start(f_st[:, o, :], wl_scr[o * P:(o + 1) * P, :]).then_inc(f_ld, 16)

            sp.wait_ge(acc_done, 2 * KT * GROUPS)
            for t in range(GT):
                sp.wait_ge(x2_stored[t], 16 * GROUPS)
            sp.dma_start(bias_bc[:, :], bias.rearrange("(a n) -> a n", a=1).to_broadcast([P, D])).then_inc(bias_ld, 16)
            for n in range(2):
                sp.dma_start(x2_st[:, n, :], x2_scr[n * P:(n + 1) * P, :]).then_inc(x2_ld[n], 16)

            def stage5_batch(b, last):
                for j in range(2):
                    n = 2 * b + j
                    if not last:
                        sp.wait_ge(x2b_ready, n + 1)
                        sp.wait_ge(x2ps_ready, 2 * n + 2)
                        sp.dma_start(x2_st[:, j, :], x2_scr[bass.ds((n + 2) * P, P), :]).then_inc(x2_ld[j], 16)
                    sp.wait_ge(y3_ready, n + 1)
                    sp.dma_start(ot[bass.ds(n * P, P), :], y3[:, j, :]).then_inc(out_stored[j], 16)
            with sp.Fori(0, BATCH - 1) as b:
                stage5_batch(b, False)
            stage5_batch(BATCH - 1, True)
            sp.wait_ge(out_stored[0], 16 * BATCH)
            sp.wait_ge(out_stored[1], 16 * BATCH)

        @block.tensor
        def _(pe):
            def product(o, l_hi, l_lo, r_hi, r_lo, first, last):
                nc.tensor.matmul(o, l_hi, r_hi, start=first, stop=False)
                nc.tensor.matmul(o, l_hi, r_lo, start=False, stop=False)
                return nc.tensor.matmul(o, l_lo, r_hi, start=False, stop=last)

            def turn(src, slot, ready):
                for h in range(2):
                    for i in range(4):
                        kt = 4 * h + i
                        mm = nc.tensor.transpose(XPS[h][:, i * P:(i + 1) * P], src[:, slot, kt * P:(kt + 1) * P],
                                                 ident[:, :])
                    mm.then_inc(ready, 1)

            def stage1_batch(b, last):
                for j in range(2):
                    n = 2 * b + j
                    pe.wait_ge(xT_lo_ready, n + 1)
                    for c in range(3):
                        wait(pe, raw_ready[c], n)
                        for kt in range(KT):
                            if c == 0 and j == 0:
                                pe.wait_ge(w_lo_ready, kt + 1)
                            mm = product(CHUNK_BANK[c][:, :], xT_hi[:, j, kt, :], xT_lo[:, j, kt, :],
                                         w_hi[:, kt, c * BANK:(c + 1) * BANK], w_lo[:, kt, c * BANK:(c + 1) * BANK],
                                         kt == 0, kt == KT - 1)
                        mm.then_inc(qkv_done[c], 1)
                        if c == 0 and not (last and j == 1):
                            if j == 0:
                                pe.wait_ge(x_ld[1], 16 * b + 16)
                            else:
                                pe.wait_ge(x_ld[0], 16 * b + 32)
                            pe.wait_ge(xT_lo_ready, n + 1)
                            turn(x_st, 1 - j, xps_ready)
                    for g, (lo, hi) in enumerate(QBLK):
                        pe.wait_ge(turned_ready[g], n + 1)
                        wait(pe, qT_lo_ready, n)
                        for i in range(lo, hi):
                            mm = nc.tensor.transpose(QPS[g][:, (i - lo) * P:(i - lo + 1) * P],
                                                     turned[:, i * P:(i + 1) * P], ident[:, :])
                        mm.then_inc(qps_ready[g], 1)

            pe.wait_ge(consts_done, 1)
            pe.wait_ge(x_ld[0], 16)
            turn(x_st, 0, xps_ready)
            stage1_batch(0, False)
            with pe.Fori(1, BATCH - 1) as b:
                stage1_batch(b, False)
            stage1_batch(BATCH - 1, True)

            def scores(b, k):
                u, pos, unit = SUB * b + k, k % 3, k // 3
                q, e, o = unit // 2, unit % 2, SBANK[pos]
                if k % 6 == 0:
                    pe.wait_ge(chunk_ld[q], 7 * 16 * (b + 1))
                wait(pe, exp_done, u - 2)
                hs, keys = heads_of(pos), keys_of(pos)
                t0 = P if pos < 2 else 0
                for i, h in enumerate(hs):
                    nc.tensor.matmul(o[:, i * keys:(i + 1) * keys], q3[:, q, REP * e + h, t0:t0 + P],
                                     k3[:, q, e, 0:keys], start=i == 0, stop=False, skip_group_check=True)
                diag = o[:, 0:len(hs) * keys].rearrange("p (h t) -> p h t", t=keys)[:, :, keys - P:keys]
                nc.tensor.matmul(diag, ident_r[:, :], mask_r[:, 0:len(hs), :], start=False, stop=True,
                                 skip_group_check=True).then_inc(s_done, 1)

            def turn_probs(b, k):
                u, pos = SUB * b + k, k % 3
                pe.wait_ge(prob_ready, u + 1)
                taken(b, k - 2)
                tb = TBANK[k % 2]
                blocks = [(t, i) for t in range(keys_of(pos) // P) for i in range(len(heads_of(pos)))]
                for at, (t, i) in enumerate(blocks):
                    c = i * keys_of(pos) + t * P
                    mm = nc.tensor.transpose(tb[:, at * P:(at + 1) * P], prob[:, k % 4, c:c + P], ident[:, :])
                mm.then_inc(pT_done, 1)

            def taken(b, k):
                if isinstance(b, int) and SUB * b + k < 0:
                    return
                unit, pos = KVH * b + k // 3, k % 3
                if pos == 1:
                    pe.wait_ge(pT_dve, unit + 1)
                else:
                    pe.wait_ge(pT_act, 2 * unit + (1 if pos == 0 else 2))

            def weighted(b, k):
                pos, unit = k % 3, k // 3
                if pos == 0:
                    return
                taken(b, k - 1)
                taken(b, k)
                q, e = unit // 2, unit % 2
                vv = vch[:, q, :, e * HD:(e + 1) * HD]
                if pos == 1:
                    wait(pe, att_ready, KVH * b + unit)
                    for t in range(2):
                        for h in range(REP):
                            src = probT[:, h // 2, (2 * t + h % 2) * P:(2 * t + h % 2 + 1) * P]
                            nc.tensor.matmul(OBANK[HD * h:HD * (h + 1), P:2 * P], vv[:, t, :], src,
                                             start=t == 0, stop=t == 1, skip_group_check=True)
                else:
                    for h in range(REP):
                        mm = nc.tensor.matmul(OBANK[HD * h:HD * (h + 1), 0:P], vv[:, 0, :],
                                              probT[:, 2, h * P:(h + 1) * P], start=True, stop=True,
                                              skip_group_check=True)
                    mm.then_inc(pv_done, 1)

            WO = [(g, kt, ps) for g in range(4) for kt in range(KT) for ps in range(3)]

            def project(b, part):
                for g, kt, ps in part:
                    st, half = g // 2, g % 2
                    o = WBANK[g % 2]
                    if g >= 2 and kt == 0 and ps == 0:
                        pe.wait_ge(y1_part, 4 * b + g - 1)
                    if g == 0 and kt % 2 == 0 and ps == 0:
                        pe.wait_ge(att_lo_ready, 4 * b + kt // 2 + 1)
                    if g == 0 and ps == 0:
                        pe.wait_ge(wo_lo_ready, kt + 1)
                    lt = att_lo if ps == 2 else att_hi
                    rt = wo_lo if ps == 1 else wo_hi
                    mm = nc.tensor.matmul(o[:, :], lt[:, kt, st * P:(st + 1) * P], rt[:, kt, half * BANK:(half + 1) * BANK],
                                          start=kt == 0 and ps == 0, stop=kt == KT - 1 and ps == 2)
                    if kt == KT - 1 and ps == 2:
                        mm.then_inc(wo_done, 1)

            def stage2_batch(b, first):
                steps = WO_LAST - WO_FIRST + 1
                for k in range(SUB):
                    scores(b, k)
                    if not first and WO_FIRST <= k <= WO_LAST:
                        i = k - WO_FIRST
                        project(b - 1, WO[len(WO) * i // steps:len(WO) * (i + 1) // steps])
                    if not (first and k < LAG):
                        late(b, k - LAG, turn_probs)
                    if not (first and k < LAG + 1):
                        late(b, k - LAG - 1, weighted)

            def late(b, k, what):
                what(b - 1, k + SUB) if k < 0 else what(b, k)

            stage2_batch(0, True)
            with pe.Fori(1, BATCH) as b:
                stage2_batch(b, False)
            for k in range(SUB, SUB + LAG + 1):
                if k - LAG < SUB:
                    turn_probs(BATCH - 1, k - LAG)
                weighted(BATCH - 1, k - LAG - 1)
            project(BATCH - 1, WO)

            pe.wait_ge(bpart_ready, 1)
            pe.wait_ge(sel0_ready, 2)
            nc.tensor.matmul(bank[5][:, 0:1], sel0[:, :], b_part[:, :], start=True, stop=True).then_inc(cps_done, 1)

            def fold(m, slot):
                pe.wait_ge(wk_lo_ready, m + 1)
                for half in range(2):
                    wait(pe, m_lo_ready, 2 * m + half - 3)
                    for dt in range(KT):
                        mm = product(bank[2 * slot + half][:, :], wk_hi[:, slot, dt, :], wk_lo[:, slot, dt, :],
                                     wq_hi[:, dt, half * BANK:(half + 1) * BANK],
                                     wq_lo[:, dt, half * BANK:(half + 1) * BANK], dt == 0, dt == KT - 1)
                    mm.then_inc(m_done, 1)
                wait(pe, ucol_ready, m)
                for dt in range(KT):
                    nc.tensor.matmul(bank[6][:, 0:2], wk_hi[:, slot, dt, :], b_hl[:, 0, dt, :], start=dt == 0, stop=False)
                    mm = nc.tensor.matmul(bank[6][:, 0:2], wk_lo[:, slot, dt, :], b_hl[:, 0, dt, :], start=False,
                                          stop=dt == KT - 1)
                mm.then_inc(u_done, 1)

            pe.wait_ge(blo_ready, 1)
            for dt in range(KT):
                pe.wait_ge(wq_lo_ready, dt + 1)
            for it in range(KT):
                for dt in range(KT):
                    o = bank[7][:, 2 * it:2 * it + 2]
                    nc.tensor.matmul(o, wq_hi[:, dt, it * P:(it + 1) * P], b_hl[:, 1, dt, :], start=dt == 0, stop=False)
                    mm = nc.tensor.matmul(o, wq_lo[:, dt, it * P:(it + 1) * P], b_hl[:, 1, dt, :], start=False,
                                          stop=dt == KT - 1)
            mm.then_inc(bA_done, 1)
            fold(0, 0)
            fold(1, 1)
            with pe.Fori(1, KT // 2) as m2:
                fold(2 * m2, 0)
                fold(2 * m2 + 1, 1)

            TPS, ACC, SPS, PPS, DPS = (bank[0], bank[1]), (bank[2], bank[3]), (bank[4], bank[5]), bank[6], bank[7]
            pe.wait_ge(m_lo_ready, 2 * KT)
            pe.wait_ge(upad_ready, 1)
            pe.wait_ge(bA_ready, 1)
            pe.wait_ge(cD_ready, 1)

            def cross_group(g2, a):
                g = 2 * g2 + a

                def turn_ctx(kt):
                    pe.wait_ge(tps_free, 16 * g + kt + 1)
                    for t in range(GT):
                        mm = nc.tensor.transpose(TPS[kt % 2][:, t * P:(t + 1) * P], ctx_st[:, a, t, kt * P:(kt + 1) * P],
                                                 ident[:, :])
                    mm.then_inc(tps_ready, 1)

                def turn_x1(t):
                    pe.wait_ge(x1_ld[t], 16 * g + 16)
                    for h in range(2):
                        pe.wait_ge(tps_free, 16 * g + 8 + 2 * t + h + 1)
                        for i in range(4):
                            kt = 4 * h + i
                            mm = nc.tensor.transpose(TPS[h][:, i * P:(i + 1) * P], x1_st[:, t, kt * P:(kt + 1) * P],
                                                     ident[:, :])
                        mm.then_inc(tps_ready, 1)

                def keys(it, kt):
                    if kt == 0:
                        pe.wait_ge(acc_free, 16 * g + it + 1)
                    mm = product(ACC[it % 2][:, :], m_hi[:, kt, it * P:(it + 1) * P], m_lo[:, kt, it * P:(it + 1) * P],
                                 cT_hi[:, kt, :], cT_lo[:, kt, :], kt == 0, kt == KT - 1)
                    if kt == KT - 1:
                        mm.then_inc(acc_done, 1)

                def scores2(t):
                    e = t // 2
                    pe.wait_ge(tps_free, 16 * g + KT + 2 * t + 4)
                    if t == 0:
                        pe.wait_ge(acc_free, 16 * g + KT + 2)
                        pe.wait_ge(d_lo_ready, g + 1)
                    pe.wait_ge(exp2_done, GT * g + t + 1)
                    o, s = SPS[t % 2][:, 0:SEQ], slice(e * SEQ, (e + 1) * SEQ)
                    for kt in range(KT):
                        product(o, x1T_hi[:, kt, :], x1T_lo[:, kt, :], k_hi[:, kt, s], k_lo[:, kt, s], kt == 0, False)
                    nc.tensor.matmul(o, ones_r[:, :], d_hi[:, s], start=False, stop=False)
                    nc.tensor.matmul(o, ones_r[:, :], d_lo[:, s], start=False, stop=True).then_inc(s2_done, 1)

                def turn_probs2(t):
                    pe.wait_ge(exp2_done, GT * g + t + 3)
                    for i in range(2):
                        mm = nc.tensor.transpose(PPS[:, i * P:(i + 1) * P], pc[:, t % 2, i * P:(i + 1) * P], ident[:, :])
                    mm.then_inc(p2T_done, 1)

                def attended(t):
                    e = t // 2
                    pe.wait_ge(p2T_ready, GT * g + t + 1)
                    for half in range(2):
                        use = KT + 2 * t + half
                        pe.wait_ge(acc_free, 16 * g + use + 1)
                        for i in range(2):
                            mm = nc.tensor.matmul(ACC[use % 2][:, :], pcT[:, t % 2, i, :],
                                                  ctx_st[:, a, 2 * e + i, half * BANK:(half + 1) * BANK],
                                                  start=i == 0, stop=i == 1)
                        mm.then_inc(acc_done, 1)

                pe.wait_ge(ctx_ld[a], GT * 16 * (g2 + 1))
                turn_ctx(0)
                turn_ctx(1)
                for kt in range(KT):
                    pe.wait_ge(tps_free, 16 * g + kt + 3)
                    keys(0, kt)
                    if kt + 2 < KT:
                        turn_ctx(kt + 2)
                for it in range(1, KT):
                    for kt in range(KT):
                        keys(it, kt)
                    if it == 5:
                        turn_x1(0)
                for kt in range(KT):
                    nc.tensor.matmul(DPS[:, :], u_pad[:, kt, :], cT_hi[:, kt, :], start=kt == 0, stop=False)
                    mm = nc.tensor.matmul(DPS[:, :], u_pad[:, kt, :], cT_lo[:, kt, :], start=False, stop=kt == KT - 1)
                mm.then_inc(d_done, 1)
                scores2(0)
                turn_x1(1)
                scores2(1)
                turn_x1(2)
                turn_probs2(0)
                attended(0)
                scores2(2)
                turn_x1(3)
                turn_probs2(1)
                attended(1)
                scores2(3)
                for t in (2, 3):
                    turn_probs2(t)
                    attended(t)

            with pe.Fori(0, GROUPS // 2) as g2:
                cross_group(g2, 0)
                cross_group(g2, 1)

            for use in range(2 * KT):
                it, half = use % KT, use // KT
                pe.wait_ge(f_ld, 16 * KT) if use == 0 else None
                if use < 2:
                    pe.wait_ge(tps_free, 16 * GROUPS + 2)
                wait(pe, f_lo_ready, use - 1)
                for i in range(4):
                    mm = nc.tensor.transpose(bank[use % 2][:, i * P:(i + 1) * P],
                                             f_st[:, 4 * half + i, it * P:(it + 1) * P], ident[:, :])
                mm.then_inc(fps_done, 1)
            pe.wait_ge(x2_ld[0], 16)
            turn(x2_st, 0, x2ps_ready)
            pe.wait_ge(f_lo_ready, 2 * KT)

            def ffn_batch(b, last):
                for j in range(2):
                    n = 2 * b + j
                    pe.wait_ge(x2T_lo_ready, n + 1)
                    for half in range(2):
                        o = bank[5 + half]
                        wait(pe, y3_part, 2 * n)
                        for kt in range(KT):
                            mm = product(o[:, :], x2T_hi[:, j, kt, :], x2T_lo[:, j, kt, :],
                                         f_hi[:, kt, half * BANK:(half + 1) * BANK],
                                         f_lo[:, kt, half * BANK:(half + 1) * BANK], kt == 0, kt == KT - 1)
                        mm.then_inc(ffn_done, 1)
                        if half == 0 and not (last and j == 1):
                            if j == 0:
                                pe.wait_ge(x2_ld[1], 16 * b + 16)
                            else:
                                pe.wait_ge(x2_ld[0], 16 * b + 32)
                            turn(x2_st, 1 - j, x2ps_ready)
            ffn_batch(0, False)
            with pe.Fori(1, BATCH - 1) as b:
                ffn_batch(b, False)
            ffn_batch(BATCH - 1, True)

        @block.scalar
        def _(act):
            nc.scalar.preload_act_table(ACT.Exp)

            def copy(o, i):
                return nc.scalar.activation(o, i, ACT.Copy)

            def x_high(n, slot, src, dst, ready, hi_ready, free, free_at):
                wait(act, free, free_at)
                for h in range(2):
                    act.wait_ge(ready, 2 * n + h + 1)
                    copy(dst[:, slot, 4 * h:4 * h + 4, :].rearrange("p k s -> p (k s)"), src[h][:, :]).then_inc(hi_ready, 1)

            x_high(0, 0, XPS, xT_hi, xps_ready, xT_hi_ready, qkv_done[2], 0)
            for kt in range(KT):
                act.wait_ge(w_ld[kt % 2], 16 * (kt // 2 + 1))
                src = w_st[:, kt % 2, :]
                copy(w_hi[:, kt, KCOLS:ROPE], src[:, 0:HEADS * HD])
                copy(w_hi[:, kt, :].rearrange("p (s c) -> p s c", c=KCOLS)[:, 0:QKV // KCOLS:QKV // KCOLS - 1, :],
                     src[:, HEADS * HD:QKV].rearrange("p (s c) -> p s c", c=KCOLS)).then_inc(w_hi_ready, 1)

            def stage1_batch(b, last):
                for j in range(2):
                    n = 2 * b + j
                    for c in range(3):
                        act.wait_ge(qkv_done[c], n + 1)
                        wait(act, cos_done[c], n)
                        wait(act, sin_done[c], n)
                        lo, hi = c * BANK, min((c + 1) * BANK, ROPE)
                        mm = copy(raw[:, lo:hi], CHUNK_BANK[c][:, 0:hi - lo])
                        if c == 2:
                            wait(act, v_stored[j], 16 * b)
                            mm = copy(v_st[:, j, :], CHUNK_BANK[c][:, hi - lo:BANK])
                        mm.then_inc(raw_ready[c], 1)
                        if c == 0 and not (last and j == 1):
                            x_high(n + 1, 1 - j, XPS, xT_hi, xps_ready, xT_hi_ready, qkv_done[2], n)
                    for g, (lo, hi) in enumerate(QBLK):
                        act.wait_ge(qps_ready[g], n + 1)
                        if g == 0:
                            wait(act, qhi_st, 16 * n)
                        copy(qT_hi[:, lo:hi, :].rearrange("p c s -> p (c s)"), QPS[g][:, 0:(hi - lo) * P])\
                            .then_inc(qT_hi_ready, 1)

            stage1_batch(0, False)
            with act.Fori(1, BATCH - 1) as b:
                stage1_batch(b, False)
            stage1_batch(BATCH - 1, True)

            def exponent(b, k):
                u, pos = SUB * b + k, k % 3
                act.wait_ge(nmax_ready, u + 1)
                wait(act, pT_done, u - 3)
                wait(act, rinv_ready, u - 3)
                keys, n = keys_of(pos), len(heads_of(pos))
                for i in range(n):
                    mm = nc.scalar.activation(prob[:, k % 4, i * keys:(i + 1) * keys], SBANK[pos][:, i * keys:(i + 1) * keys],
                                              ACT.Exp, bias=nmax[:, k % 4, i:i + 1], accum_out=rsum[:, k % 4, i:i + 1])
                mm.then_inc(exp_done, 1)

            def probs_out(b, k):
                u, pos, unit = SUB * b + k, k % 3, KVH * b + k // 3
                if pos == 1:
                    return
                act.wait_ge(pT_done, u + 1)
                wait(act, pv_done, unit)
                copy(probT[:, pos, :], TBANK[k % 2][:, :]).then_inc(pT_act, 1)

            def att_high(b, pair):
                wait(act, att_ready, KVH * b + 2 * pair + 2)
                copy(att_hi[:, 2 * pair:2 * pair + 2, :].rearrange("p k s -> p (k s)"),
                     att[:, 2 * pair:2 * pair + 2, :].rearrange("p k s -> p (k s)")).then_inc(att_hi_ready, 1)

            def late(b, k, what):
                what(b - 1, k + SUB) if k < 0 else what(b, k)

            def stage2_batch(b, first):
                for k in range(SUB):
                    exponent(b, k)
                    if not first and k in SPLIT_STEP:
                        att_high(b - 1, SPLIT_STEP[k])
                    if not (first and k < LAG):
                        late(b, k - LAG, probs_out)
                    if first and k % 2 == 0 and 2 <= k <= 2 * KT:
                        kt = k // 2 - 1
                        act.wait_ge(wo_ld[kt % 2], 16 * (kt // 2 + 1))
                        copy(wo_hi[:, kt, :], wo_st[:, kt % 2, :]).then_inc(wo_hi_ready, 1)

            stage2_batch(0, True)
            with act.Fori(1, BATCH) as b:
                stage2_batch(b, False)
            for k in range(SUB - LAG, SUB):
                probs_out(BATCH - 1, k)
            for pair in range(4):
                att_high(BATCH - 1, pair)

            act.wait_ge(b_ld, 32)
            copy(b_hl[:, :, :, 0], b_raw[:, :, :]).then_inc(bhi_ready, 1)

            def wk_high(m, slot, uses):
                act.wait_ge(wk_ld[slot], 16 * uses)
                wait(act, u_done, m - 1)
                copy(wk_hi[:, slot, :, :], wk_st[:, slot, :, :]).then_inc(wk_hi_ready, 1)

            def m_high(m, slot):
                for half in range(2):
                    act.wait_ge(m_done, 2 * m + half + 1)
                    copy(m_hi[:, bass.ds(m, 1), half * BANK:(half + 1) * BANK],
                         bank[2 * slot + half][:, :].unsqueeze(1)).then_inc(m_hi_ready, 1)
            wk_high(0, 0, 1)
            wk_high(1, 1, 1)
            for dt in range(KT):
                act.wait_ge(wq_ld[dt % 2], 16 * (dt // 2 + 1))
                copy(wq_hi[:, dt, :], wq_st[:, dt % 2, :]).then_inc(wq_hi_ready, 1)
            act.wait_ge(cps_done, 1)
            copy(cD[:, :], bank[5][:, 0:1]).then_inc(cD_ready, 1)
            with act.Fori(0, KT // 2 - 1) as m2:
                m_high(2 * m2, 0)
                wk_high(2 * m2 + 2, 0, m2 + 2)
                m_high(2 * m2 + 1, 1)
                wk_high(2 * m2 + 3, 1, m2 + 2)
            m_high(KT - 2, 0)
            m_high(KT - 1, 1)
            act.wait_ge(ucol_ready, KT)
            act.wait_ge(sel0_ready, 3)
            copy(u_pad[:, :, 0], u_col[:, :]).then_inc(uhi_ready, 1)

            TPS, ACC, SPS, PPS, DPS = (bank[0], bank[1]), (bank[2], bank[3]), (bank[4], bank[5]), bank[6], bank[7]
            act.wait_ge(m_lo_ready, 2 * KT)
            act.wait_ge(upad_ready, 1)
            act.wait_ge(bA_ready, 1)
            act.sem_inc(exp2_done, 2)

            def cross_group(g2, a):
                g = 2 * g2 + a

                def ctx_high(kt):
                    act.wait_ge(tps_ready, 16 * g + kt + 1)
                    copy(cT_hi[:, kt, :], TPS[kt % 2][:, :]).then_inc(cT_hi_ready, 1)

                def key_high(it):
                    act.wait_ge(acc_done, 16 * g + it + 1)
                    nc.scalar.activation(k_hi[:, it, :], ACC[it % 2][:, :], ACT.Identity, bias=bA[:, it:it + 1])\
                        .then_inc(k_hi_ready, 1)

                def x1_high(t):
                    if t:
                        act.wait_ge(s2_done, GT * g + t)
                    for h in range(2):
                        act.wait_ge(tps_ready, 16 * g + 8 + 2 * t + h + 1)
                        copy(x1T_hi[:, 4 * h:4 * h + 4, :].rearrange("p k s -> p (k s)"), TPS[h][:, :])\
                            .then_inc(x1T_hi_ready, 1)

                def exponent2(t):
                    act.wait_ge(nmax2_ready, GT * g + t + 1)
                    act.wait_ge(p2T_done, GT * g + t + 1)
                    nc.scalar.activation(pc[:, t % 2, :], SPS[t % 2][:, 0:SEQ], ACT.Exp, bias=nm2[:, t, 1:2],
                                         scale=CROSS_SCALE, accum_out=rs2[:, t:t + 1]).then_inc(exp2_done, 1)

                def probs_out2(t):
                    act.wait_ge(p2T_done, GT * g + t + 3)
                    act.wait_ge(acc_done, 16 * g + KT + 2 * t - 2)
                    copy(pcT[:, t % 2, :, :].rearrange("p i s -> p (i s)"), PPS[:, 0:2 * P]).then_inc(p2T_ready, 1)

                for kt in range(KT):
                    ctx_high(kt)
                for it in range(KT):
                    key_high(it)
                    if it == 5:
                        x1_high(0)
                act.wait_ge(d_done, g + 1)
                nc.scalar.activation(d_hi[:, :], DPS[:, :], ACT.Identity, bias=cD[:, :]).then_inc(d_hi_ready, 1)
                x1_high(1)
                exponent2(0)
                x1_high(2)
                exponent2(1)
                probs_out2(0)
                x1_high(3)
                exponent2(2)
                probs_out2(1)
                exponent2(3)
                probs_out2(2)
                probs_out2(3)

            with act.Fori(0, GROUPS // 2) as g2:
                cross_group(g2, 0)
                cross_group(g2, 1)

            for use in range(2 * KT):
                it, half = use % KT, use // KT
                act.wait_ge(fps_done, use + 1)
                copy(f_hi[:, it, half * BANK:(half + 1) * BANK], bank[use % 2][:, :]).then_inc(f_hi_ready, 1)
            x_high(0, 0, XPS, x2T_hi, x2ps_ready, x2T_hi_ready, ffn_done, 0)

            def ffn_batch(b, last):
                for j in range(2):
                    n = 2 * b + j
                    if not (last and j == 1):
                        x_high(n + 1, 1 - j, XPS, x2T_hi, x2ps_ready, x2T_hi_ready, ffn_done, 2 * n)
            ffn_batch(0, False)
            with act.Fori(1, BATCH - 1) as b:
                ffn_batch(b, False)
            ffn_batch(BATCH - 1, True)

        @block.vector
        def _(dve):
            def low(o, i, hi):
                return nc.vector.tensor_tensor(o, i, hi.bitcast(F32), ALU.subtract)

            def x_low(n, slot, src, dst_hi, dst_lo, hi_ready, ready):
                for h in range(2):
                    dve.wait_ge(hi_ready, 2 * n + h + 1)
                    flat = lambda w: w[:, slot, 4 * h:4 * h + 4, :].rearrange("p k s -> p (k s)")
                    mm = low(flat(dst_lo), src[h][:, :], flat(dst_hi))
                mm.then_inc(ready, 1)

            x_low(0, 0, XPS, xT_hi, xT_lo, xT_hi_ready, xT_lo_ready)
            for kt in range(KT):
                dve.wait_ge(w_hi_ready, kt + 1)
                src = w_st[:, kt % 2, :]
                low(w_lo[:, kt, KCOLS:ROPE], src[:, 0:HEADS * HD], w_hi[:, kt, KCOLS:ROPE])
                ends = lambda w: w[:, kt, :].rearrange("p (s c) -> p s c", c=KCOLS)[:, 0:QKV // KCOLS:QKV // KCOLS - 1, :]
                low(ends(w_lo), src[:, HEADS * HD:QKV].rearrange("p (s c) -> p s c", c=KCOLS), ends(w_hi))\
                    .then_inc(w_lo_ready, 1)

            def sines(n, j, c):
                dve.wait_ge(raw_ready[c], n + 1)
                wait(dve, turned_ready[c], n)
                for lo, hi, ty in PIECE[c]:
                    pair = lambda w, i: w[:, lo:hi].rearrange("p (h d i) -> p h d i", i=2, d=HD // 2)[:, :, :, i]
                    nh = (hi - lo) // HD
                    for i, at in ((0, HD), (1, HD + HD // 2)):
                        sn = tab[:, j, ty, at:at + HD // 2].unsqueeze(1).to_broadcast([P, nh, HD // 2])
                        mm = nc.vector.tensor_tensor(pair(rot_s, i), pair(raw, 1 - i), sn, ALU.mult)
                mm.then_inc(sin_done[c], 1)

            A, B, C, T = pick

            def decode(b):
                def spread(s0, s1):
                    def go():
                        if s0 == 0:
                            dve.wait_ge(code_ld, 32 * b + 32)
                        for s in range(s0, s1):
                            mm = nc.vector.tensor_scalar(bits[:, :, :].rearrange("p q (w s) -> p q w s", s=32)[:, :, :, s],
                                                         planes[:, :, :], 31 - s, 31, ALU.logical_shift_left,
                                                         ALU.arith_shift_right)
                        if s1 == 32:
                            mm.then_inc(bits_ready, 1)
                            nc.vector.tensor_tensor(lut_x[:, :], lut[:, 0:LEVELS:2].bitcast(I32),
                                                    lut[:, 1:LEVELS:2].bitcast(I32), ALU.bitwise_xor).then_inc(lutx_ready, 1)
                    return go

                count = [0]

                def leaf(o, i, after=0):
                    at = count[0]
                    count[0] += 1

                    def go():
                        if at == 0:
                            dve.wait_ge(bits_ready, b + 1)
                            dve.wait_ge(lutx_ready, b + 1)
                            wait(dve, wl_stored, 16 * b)
                        if after:
                            dve.wait_ge(pick_step, PICKS * b + after)
                        nc.vector.tensor_scalar(o[:, :], bits[:, 0, :], lut_x[:, i:i + 1],
                                                lut[:, 2 * i:2 * i + 1].bitcast(I32), ALU.bitwise_and, ALU.bitwise_xor)\
                            .then_inc(pick_step, 1)
                    return go

                def choose(o, bit, other):
                    at = count[0]
                    count[0] += 1

                    def go():
                        wait_alone(dve, pick_step, PICKS * b + at)
                        nc.vector.copy_predicated(o[:, :], bits[:, bit, :], other[:, :]).then_inc(pick_step, 1)
                    return go

                tree = [leaf(A, 0), leaf(B, 1), choose(A, 1, B), leaf(B, 2, 3), leaf(C, 3), choose(B, 1, C), choose(A, 2, B),
                        leaf(B, 4, 7), leaf(C, 5), choose(B, 1, C), leaf(C, 6, 10), leaf(T, 7), choose(C, 1, T), choose(B, 2, C),
                        choose(A, 3, B)]
                return [spread(0, 12), spread(12, 26), spread(26, 32)] + [tree[0:6], tree[6:11], tree[11:15]]

            def run(steps):
                for go in (steps if isinstance(steps, list) else [steps]):
                    go()

            def stage1_batch(b, last):
                parts = decode(b)
                for j in range(2):
                    n = 2 * b + j
                    sines(n, j, 0)
                    if not (last and j == 1):
                        x_low(n + 1, 1 - j, XPS, xT_hi, xT_lo, xT_hi_ready, xT_lo_ready)
                    run(parts[3 * j])
                    sines(n, j, 1)
                    run(parts[3 * j + 1])
                    sines(n, j, 2)
                    for g, (lo, hi) in enumerate(QBLK):
                        dve.wait_ge(qT_hi_ready, 3 * n + g + 1)
                        if g == 0:
                            wait(dve, qlo_st, 16 * n)
                        flat = lambda w: w[:, lo:hi, :].rearrange("p c s -> p (c s)")
                        mm = low(flat(qT_lo), QPS[g][:, 0:(hi - lo) * P], flat(qT_hi))
                    mm.then_inc(qT_lo_ready, 1)
                    run(parts[3 * j + 2])

            dve.wait_ge(tab_ld, 16)
            stage1_batch(0, False)
            with dve.Fori(1, BATCH - 1) as b:
                stage1_batch(b, False)
            stage1_batch(BATCH - 1, True)

            def maxima(b, k):
                u, pos = SUB * b + k, k % 3
                dve.wait_ge(s_done, u + 1)
                wait(dve, exp_done, u - 3)
                n, keys = len(heads_of(pos)), keys_of(pos)
                nc.vector.tensor_reduce(nmax[:, k % 4, 0:n], SBANK[pos][:, :].rearrange("p (h t) -> p h t", t=keys),
                                        axis=AX.X, op=ALU.max, negate=True).then_inc(nmax_ready, 1)

            def inverse(b, k):
                u, n = SUB * b + k, len(heads_of(k % 3))
                dve.wait_ge(exp_done, u + 1)
                wait(dve, prob_ready, u - 3)
                nc.vector.reciprocal(rinv[:, k % 4, 0:n], rsum[:, k % 4, 0:n]).then_inc(rinv_ready, 1)

            def probs_out(b, k):
                u, pos, unit = SUB * b + k, k % 3, KVH * b + k // 3
                if pos == 1:
                    dve.wait_ge(pT_done, u + 1)
                    wait(dve, pv_done, unit)
                    nc.vector.tensor_copy(probT[:, pos, :], TBANK[k % 2][:, :]).then_inc(pT_dve, 1)

            def out_unit(b, k, behind):
                unit = k // 3
                if k % 3 == 2:
                    dve.wait_ge(pv_done, KVH * b + unit + 1)
                    if behind:
                        dve.wait_ge(att_hi_ready, 4 * (b - 1) + unit // 2 + 1)
                    nc.vector.tensor_copy(att[:, unit, :], OBANK[:, 0:SEQ]).then_inc(att_ready, 1)

            def att_low(b, pair):
                dve.wait_ge(att_hi_ready, 4 * b + pair + 1)
                flat = lambda w: w[:, 2 * pair:2 * pair + 2, :].rearrange("p k s -> p (k s)")
                low(flat(att_lo), flat(att), flat(att_hi)).then_inc(att_lo_ready, 1)

            def add_part(b, g):
                st, half = g // 2, g % 2
                cols = slice(half * BANK, (half + 1) * BANK)
                dve.wait_ge(wo_done, 4 * b + g + 1)
                if half == 0:
                    dve.wait_ge(xr_ld[st], 16 * b + 16)
                    dve.wait_ge(x1_stored[st], 16 * b + 16)
                nc.vector.tensor_tensor(y1[:, st, cols], WBANK[g % 2][:, :], xr[:, st, cols], ALU.add).then_inc(y1_part, 1)
                dve.wait_ge(y1_part, 4 * b + g + 1)
                nc.vector.bn_stats(st1[:, st, half, :], y1[:, st, cols]).then_inc(y1_stats, 1)
                if half == 1:
                    wait_alone(dve, y1_stats, 4 * b + g + 1)
                    nc.vector.bn_aggr(mv1[:, st, :], st1[:, st, :, :].rearrange("p h s -> p (h s)")).then_inc(y1_mv, 1)
                    dve.wait_ge(y1_mv, 2 * b + st + 1)
                    nc.vector.tensor_scalar_add(rs1[:, st, 0:1], mv1[:, st, 1:2], EPS).then_inc(y1_var, 1)

            def normalise(b, st):
                dve.wait_ge(y1_rstd, 2 * b + st + 1)
                nc.vector.tensor_scalar(y1[:, st, :], y1[:, st, :], mv1[:, st, 0:1], rs1[:, st, 1:2], ALU.subtract,
                                        ALU.mult).then_inc(y1_ready, 1)

            def late(b, k, what, *more):
                what(b - 1, k + SUB, *more) if k < 0 else what(b, k, *more)

            def stage2_batch(b, first):
                for k in range(SUB):
                    maxima(b, k)
                    if not (first and k < 1):
                        late(b, k - 1, inverse)
                    if not (first and k < LAG):
                        late(b, k - LAG, probs_out)
                    if not (first and k < LAG + 1):
                        if k - LAG - 1 < 0:
                            out_prev(b, k - LAG - 1 + SUB, first)
                        else:
                            out_unit(b, k - LAG - 1, not first)
                    if not first and k in SPLIT_STEP:
                        att_low(b - 1, SPLIT_STEP[k])
                    if first and k % 2 == 0 and 2 <= k <= 2 * KT:
                        kt = k // 2 - 1
                        dve.wait_ge(wo_hi_ready, kt + 1)
                        low(wo_lo[:, kt, :], wo_st[:, kt % 2, :], wo_hi[:, kt, :]).then_inc(wo_lo_ready, 1)
                    if not first:
                        if k in (11, 15, 20, 23):
                            add_part(b - 1, (11, 15, 20, 23).index(k))
                        if k == 18:
                            normalise(b - 1, 0)
                if not first:
                    normalise(b - 1, 1)

            def out_prev(b, k, first):
                unit = k // 3
                if k % 3 == 2:
                    dve.wait_ge(pv_done, KVH * (b - 1) + unit + 1)
                    nc.vector.tensor_copy(att[:, unit, :], OBANK[:, 0:SEQ]).then_inc(att_ready, 1)

            stage2_batch(0, True)
            with dve.Fori(1, BATCH) as b:
                stage2_batch(b, False)
            inverse(BATCH - 1, SUB - 1)
            for k in range(SUB, SUB + LAG + 1):
                if k - LAG < SUB:
                    probs_out(BATCH - 1, k - LAG)
                out_unit(BATCH - 1, k - LAG - 1, True)
            for pair in range(4):
                att_low(BATCH - 1, pair)
            for g in range(4):
                add_part(BATCH - 1, g)
                if g % 2:
                    normalise(BATCH - 1, g // 2)

            dve.wait_ge(b_ld, 32)
            nc.vector.tensor_tensor(b_prod[:, :], b_raw[:, 0, :], b_raw[:, 1, :], ALU.mult).then_inc(bprod_ready, 1)
            dve.wait_ge(bhi_ready, 1)
            low(b_hl[:, :, :, 1], b_raw[:, :, :], b_hl[:, :, :, 0]).then_inc(blo_ready, 1)
            dve.wait_ge(bprod_ready, 1)
            nc.vector.tensor_reduce(b_part[:, :], b_prod[:, :], axis=AX.X, op=ALU.add).then_inc(bpart_ready, 1)

            def wk_low(m, slot):
                dve.wait_ge(wk_hi_ready, m + 1)
                low(wk_lo[:, slot, :, :], wk_st[:, slot, :, :], wk_hi[:, slot, :, :]).then_inc(wk_lo_ready, 1)

            def m_low(m, slot):
                for half in range(2):
                    dve.wait_ge(m_hi_ready, 2 * m + half + 1)
                    row = lambda w: w[:, bass.ds(m, 1), half * BANK:(half + 1) * BANK]
                    low(row(m_lo), bank[2 * slot + half][:, :].unsqueeze(1), row(m_hi)).then_inc(m_lo_ready, 1)
                dve.wait_ge(u_done, m + 1)
                nc.vector.tensor_reduce(u_col[:, bass.ds(m, 1)], bank[6][:, 0:2], axis=AX.X, op=ALU.add)\
                    .then_inc(ucol_ready, 1)

            wk_low(0, 0)
            wk_low(1, 1)
            for dt in range(KT):
                dve.wait_ge(wq_hi_ready, dt + 1)
                low(wq_lo[:, dt, :], wq_st[:, dt % 2, :], wq_hi[:, dt, :]).then_inc(wq_lo_ready, 1)
            dve.wait_ge(bA_done, 1)
            nc.vector.tensor_reduce(bA[:, :], bank[7][:, 0:2 * KT].rearrange("p (t i) -> p t i", i=2), axis=AX.X, op=ALU.add)\
                .then_inc(bA_ready, 1)
            with dve.Fori(0, KT // 2 - 1) as m2:
                m_low(2 * m2, 0)
                wk_low(2 * m2 + 2, 0)
                m_low(2 * m2 + 1, 1)
                wk_low(2 * m2 + 3, 1)
            m_low(KT - 2, 0)
            m_low(KT - 1, 1)
            dve.wait_ge(uhi_ready, 1)
            low(u_pad[:, :, 1], u_col[:, :], u_pad[:, :, 0]).then_inc(upad_ready, 1)

            TPS, ACC, SPS, PPS, DPS = (bank[0], bank[1]), (bank[2], bank[3]), (bank[4], bank[5]), bank[6], bank[7]
            dve.wait_ge(cD_ready, 1)
            dve.sem_inc(tps_free, 2)
            dve.sem_inc(acc_free, 2)

            def cross_group(g2, a):
                g = 2 * g2 + a

                def ctx_low(kt):
                    dve.wait_ge(cT_hi_ready, KT * g + kt + 1)
                    low(cT_lo[:, kt, :], TPS[kt % 2][:, :], cT_hi[:, kt, :]).then_inc(tps_free, 1)

                def key_low(it):
                    dve.wait_ge(k_hi_ready, KT * g + it + 1)
                    nc.vector.scalar_tensor_tensor(out=k_lo[:, it, :], in0=ACC[it % 2][:, :], scalar=bA[:, it:it + 1],
                                                   in1=k_hi[:, it, :].bitcast(F32), op0=ALU.add, op1=ALU.subtract)\
                        .then_inc(acc_free, 1)

                def x1_low(t):
                    for h in range(2):
                        dve.wait_ge(x1T_hi_ready, 2 * (GT * g + t) + h + 1)
                        flat = lambda w: w[:, 4 * h:4 * h + 4, :].rearrange("p k s -> p (k s)")
                        low(flat(x1T_lo), TPS[h][:, :], flat(x1T_hi)).then_inc(tps_free, 1)

                def maxima2(t):
                    dve.wait_ge(s2_done, GT * g + t + 1)
                    if t == 0:
                        wait(dve, exp2_done, GT * g + 2)
                    nc.vector.tensor_reduce(nm2[:, t, 0:1], SPS[t % 2][:, 0:SEQ], axis=AX.X, op=ALU.max, negate=True)\
                        .then_inc(nmax2_raw, 1)
                    dve.wait_ge(nmax2_raw, GT * g + t + 1)
                    nc.vector.tensor_scalar_mul(nm2[:, t, 1:2], nm2[:, t, 0:1], CROSS_SCALE).then_inc(nmax2_ready, 1)

                def add_cross(t):
                    dve.wait_ge(exp2_done, GT * g + t + 3)
                    nc.vector.reciprocal(ri2[:, t:t + 1], rs2[:, t:t + 1]).then_inc(rinv2_ready, 1)
                    dve.wait_ge(rinv2_ready, GT * g + t + 1)
                    for half in range(2):
                        use, cols = KT + 2 * t + half, slice(half * BANK, (half + 1) * BANK)
                        dve.wait_ge(acc_done, 16 * g + use + 1)
                        nc.vector.scalar_tensor_tensor(out=x1_st[:, t, cols], in0=ACC[use % 2][:, :], scalar=ri2[:, t:t + 1],
                                                       in1=x1_st[:, t, cols], op0=ALU.mult, op1=ALU.add).then_inc(acc_free, 1)
                        dve.wait_ge(acc_free, 16 * g + use + 3)
                        nc.vector.bn_stats(st2[:, t, half, :], x1_st[:, t, cols]).then_inc(y2_stats, 1)
                    wait_alone(dve, y2_stats, 2 * (GT * g + t) + 2)
                    nc.vector.bn_aggr(mv2[:, t, :], st2[:, t, :, :].rearrange("p h s -> p (h s)")).then_inc(y2_mv, 1)
                    dve.wait_ge(y2_mv, GT * g + t + 1)
                    nc.vector.tensor_scalar_add(rv2[:, t, 0:1], mv2[:, t, 1:2], EPS).then_inc(y2_var, 1)

                def normalise2(t):
                    dve.wait_ge(y2_rstd, GT * g + t + 1)
                    nc.vector.tensor_scalar(x1_st[:, t, :], x1_st[:, t, :], mv2[:, t, 0:1], rv2[:, t, 1:2], ALU.subtract,
                                            ALU.mult).then_inc(y2_ready, 1)

                for kt in range(KT):
                    ctx_low(kt)
                for it in range(KT):
                    key_low(it)
                    if it == 5:
                        x1_low(0)
                dve.wait_ge(d_hi_ready, g + 1)
                nc.vector.scalar_tensor_tensor(out=d_lo[:, :], in0=DPS[:, :], scalar=cD[:, :], in1=d_hi[:, :].bitcast(F32),
                                               op0=ALU.add, op1=ALU.subtract).then_inc(d_lo_ready, 1)
                x1_low(1)
                maxima2(0)
                x1_low(2)
                maxima2(1)
                add_cross(0)
                x1_low(3)
                maxima2(2)
                normalise2(0)
                add_cross(1)
                maxima2(3)
                normalise2(1)
                add_cross(2)
                add_cross(3)
                normalise2(2)
                normalise2(3)

            with dve.Fori(0, GROUPS // 2) as g2:
                cross_group(g2, 0)
                cross_group(g2, 1)

            for use in range(2 * KT):
                it, half = use % KT, use // KT
                cols = slice(half * BANK, (half + 1) * BANK)
                dve.wait_ge(f_hi_ready, use + 1)
                low(f_lo[:, it, cols], bank[use % 2][:, :], f_hi[:, it, cols]).then_inc(f_lo_ready, 1)
            x_low(0, 0, XPS, x2T_hi, x2T_lo, x2T_hi_ready, x2T_lo_ready)

            def ffn_batch(b, last):
                for j in range(2):
                    n = 2 * b + j
                    if not (last and j == 1):
                        x_low(n + 1, 1 - j, XPS, x2T_hi, x2T_lo, x2T_hi_ready, x2T_lo_ready)
                    dve.wait_ge(x2b_ready, n + 1)
                    wait(dve, out_stored[j], 16 * b)
                    for half in range(2):
                        cols = slice(half * BANK, (half + 1) * BANK)
                        dve.wait_ge(ffn_done, 2 * n + half + 1)
                        nc.vector.tensor_tensor(y3[:, j, cols], bank[5 + half][:, :], x2b[:, j, cols], ALU.add)\
                            .then_inc(y3_part, 1)
                        dve.wait_ge(y3_part, 2 * n + half + 1)
                        nc.vector.bn_stats(st3[:, j, half, :], y3[:, j, cols]).then_inc(y3_stats, 1)
                    wait_alone(dve, y3_stats, 2 * n + 2)
                    nc.vector.bn_aggr(mv3[:, j, :], st3[:, j, :, :].rearrange("p h s -> p (h s)")).then_inc(y3_mv, 1)
                    dve.wait_ge(y3_mv, n + 1)
                    nc.vector.tensor_scalar_add(rv3[:, j, 0:1], mv3[:, j, 1:2], EPS).then_inc(y3_var, 1)
                    dve.wait_ge(y3_rstd, n + 1)
                    nc.vector.tensor_scalar(y3[:, j, :], y3[:, j, :], mv3[:, j, 0:1], rv3[:, j, 1:2], ALU.subtract,
                                            ALU.mult).then_inc(y3_ready, 1)
            ffn_batch(0, False)
            with dve.Fori(1, BATCH - 1) as b:
                ffn_batch(b, False)
            ffn_batch(BATCH - 1, True)

        @block.gpsimd
        def _(pool):
            nc.gpsimd.memset(ident[:, :], 0.0)
            nc.gpsimd.memset(rot_c[:, 0:BANK], 0.0)
            nc.gpsimd.memset(rot_c[:, BANK:BANK + P], 1.0)
            nc.gpsimd.memset(neg_half[:, :], -0.5).then_inc(consts_step, 1)
            pool.wait_ge(consts_step, 1)
            nc.gpsimd.affine_select(out=ident[:, :], in_=ident[:, :], compare_op=ALU.not_equal, fill=1.0, base=0,
                                    pattern=[[-1, P]], channel_multiplier=1).then_inc(consts_step, 1)
            m3 = rot_c[:, 0:BANK].rearrange("p (h t) -> p h t", t=P)
            nc.gpsimd.affine_select(out=m3, in_=m3, compare_op=ALU.is_ge, fill=MASKED, base=0,
                                    pattern=[[0, REP], [-1, P]], channel_multiplier=1).then_inc(consts_step, 1)
            pool.wait_ge(consts_step, 3)
            nc.gpsimd.tensor_copy(ident_r[:, :], ident[:, :])
            nc.gpsimd.tensor_copy(mask_r[:, :, :].rearrange("p h t -> p (h t)"), rot_c[:, 0:BANK])
            nc.gpsimd.tensor_copy(ones_r[:, :], rot_c[:, BANK:BANK + P]).then_inc(consts_done, 1)

            def cosines(n, j, c):
                pool.wait_ge(raw_ready[c], n + 1)
                for lo, hi, ty in PIECE[c]:
                    nh = (hi - lo) // HD
                    head = lambda w: w[:, lo:hi].rearrange("p (h d) -> p h d", d=HD)
                    cs = tab[:, j, ty, 0:HD].unsqueeze(1).to_broadcast([P, nh, HD])
                    mm = nc.gpsimd.tensor_tensor(head(rot_c), head(raw), cs, ALU.mult)
                mm.then_inc(cos_done[c], 1)

            def turned_chunk(n, c):
                lo, hi = c * BANK, min((c + 1) * BANK, ROPE)
                pool.wait_ge(cos_done[c], n + 1)
                pool.wait_ge(sin_done[c], n + 1)
                wait(pool, qps_ready[c], n)
                nc.gpsimd.tensor_tensor(turned[:, lo:hi], rot_c[:, lo:hi], rot_s[:, lo:hi], ALU.add)\
                    .then_inc(turned_ready[c], 1)

            pool.wait_ge(tab_ld, 16)
            def stage1_batch(b):
                for j in range(2):
                    for c in range(3):
                        cosines(2 * b + j, j, c)
                        turned_chunk(2 * b + j, c)

            stage1_batch(0)
            with pool.Fori(1, BATCH) as b:
                stage1_batch(b)

            def rstd1(b, st):
                pool.wait_ge(y1_var, 2 * b + st + 1)
                nc.gpsimd.tensor_tensor(rs1[:, st, 1:2], rs1[:, st, 0:1], neg_half[:, :], ALU.pow).then_inc(y1_rstd, 1)

            def scale_probs(b, k):
                u, pos = SUB * b + k, k % 3
                n, keys = len(heads_of(pos)), keys_of(pos)
                pool.wait_ge(rinv_ready, u + 1)
                pr = prob[:, k % 4, :].rearrange("p (h t) -> p h t", t=keys)
                nc.gpsimd.tensor_tensor(pr, pr, rinv[:, k % 4, 0:n].unsqueeze(2).to_broadcast([P, n, keys]), ALU.mult)\
                    .then_inc(prob_ready, 1)

            def stage2_batch(b, first):
                for k in range(SUB):
                    if not first and k == SUB - 1:
                        rstd1(b - 1, 1)
                    scale_probs(b, k)
                    if not first:
                        if k == 15:
                            rstd1(b - 1, 0)

            stage2_batch(0, True)
            with pool.Fori(1, BATCH) as b:
                stage2_batch(b, False)
            for st in range(2):
                rstd1(BATCH - 1, st)

            pool.wait_ge(b_ld, 32)
            nc.gpsimd.memset(sel0[:, :], 0.0).then_inc(sel0_ready, 1)
            pool.wait_ge(sel0_ready, 1)
            nc.gpsimd.memset(sel0[:, 0:1], 1.0).then_inc(sel0_ready, 1)
            nc.gpsimd.memset(u_pad[:, :, :].bitcast(F32), 0.0).then_inc(sel0_ready, 1)

            pool.sem_inc(p2T_done, 2)
            with pool.Fori(0, TILES // GT) as g:
                for t in range(GT):
                    pool.wait_ge(y2_var, GT * g + t + 1)
                    nc.gpsimd.tensor_tensor(rv2[:, t, 1:2], rv2[:, t, 0:1], neg_half[:, :], ALU.pow).then_inc(y2_rstd, 1)

            pool.wait_ge(bias_ld, 16)
            with pool.Fori(0, BATCH) as b:
                for j in range(2):
                    n = 2 * b + j
                    pool.wait_ge(x2_ld[j], 16 * b + 16)
                    nc.gpsimd.tensor_tensor(x2b[:, j, :], x2_st[:, j, :], bias_bc[:, :], ALU.add).then_inc(x2b_ready, 1)
                    pool.wait_ge(y3_var, n + 1)
                    nc.gpsimd.tensor_tensor(rv3[:, j, 1:2], rv3[:, j, 0:1], neg_half[:, :], ALU.pow).then_inc(y3_rstd, 1)


def kernel(x, ctx_4096, L0_attn_w_qkv, L0_attn_w_o, L0_xattn_Wq, L0_xattn_bq, L0_xattn_Wk, L0_xattn_bk, L0_ffn_qweight,
           L0_ffn_lut4, L0_ffn_lut8, L0_ffn_bias):
    import concourse.bacc as bacc
    from concourse.bass_utils import run_bass_kernel_spmd

    arrays = {"x": x, "ctx_in": ctx_4096, "w_qkv": L0_attn_w_qkv, "w_o": L0_attn_w_o, "wq": L0_xattn_Wq,
              "bq": L0_xattn_bq, "wk": L0_xattn_Wk, "bk": L0_xattn_bk, "qweight": L0_ffn_qweight, "lut4": L0_ffn_lut4,
              "bias": L0_ffn_bias, "rope": rope_tables()}
    arrays = {name: np.ascontiguousarray(a) for name, a in arrays.items()}
    nc = bacc.Bacc("TRN2", target_bir_lowering=False, num_devices=1)
    aps = {name: nc.dram_tensor(name, a.shape, mybir.dt.from_np(a.dtype), kind="ExternalInput").ap()
           for name, a in arrays.items()}
    out = nc.dram_tensor("out", (BATCH, SEQ, D), F32, kind="ExternalOutput").ap()
    decoder_layer(nc, out=out, **aps)
    r = run_bass_kernel_spmd(nc, [arrays], core_ids=[0])
    return r.results[0]["out"]
```

```python
import math
from contextlib import ExitStack

import numpy as np

import concourse.bass as bass
from concourse import mybir

F32, F32R, I32 = mybir.dt.float32, mybir.dt.float32r, mybir.dt.int32
ALU, ACT, AX = mybir.AluOpType, mybir.ActivationFunctionType, mybir.AxisListType

P = 128
BATCH, SEQ, D = 8, 256, 1024
TOK = BATCH * SEQ
TILES = TOK // P
KT = D // P
HEADS, KVH, HD = 32, 8, 32
REP = HEADS // KVH
KCOLS = KVH * HD
QKV = HEADS * HD + 2 * KCOLS
ROPE = HEADS * HD + KCOLS
RB = ROPE // P
BANK = 512
SLOTS = 4
EPS = 1e-5
MASKED = -1e30
BITS, LEVELS = 4, 16
GROUP = 512
GT = GROUP // P
GROUPS = TOK // GROUP
PICKS = 15
ACC_USES = KT + 2 * GT
CROSS_SCALE = 1.0 / math.sqrt(D)


def rope_tables():
    inv = (np.float32(1.0) / np.float32(10000.0) ** (np.arange(0, HD, 2, dtype=np.float32) / np.float32(HD)))
    ang = np.arange(SEQ, dtype=np.float32)[:, None] * inv.astype(np.float32)[None, :]
    c, s = np.cos(ang).astype(np.float32), np.sin(ang).astype(np.float32)
    one = np.concatenate([np.repeat(c, 2, axis=1), -s, s], axis=1)
    return np.ascontiguousarray(np.stack([one, one * np.float32(1.0 / math.sqrt(HD))], axis=1).astype(np.float32))


def decoder_layer(nc, x, ctx_in, w_qkv, w_o, wq, bq, wk, bk, qweight, lut4, bias, rope, out):
    qk_scr = nc.dram_tensor("qk_scr", (2, ROPE, TOK), F32, kind="Internal").ap()
    v_scr = nc.dram_tensor("v_scr", (TOK, KCOLS), F32, kind="Internal").ap()
    x1_scr = nc.dram_tensor("x1_scr", (TOK, D), F32, kind="Internal").ap()
    x2_scr = nc.dram_tensor("x2_scr", (TOK, D), F32, kind="Internal").ap()
    f_scr = nc.dram_tensor("f_scr", (2, D, D), F32, kind="Internal").ap()

    xt, cx = x.rearrange("b s d -> (b s) d"), ctx_in.rearrange("b s d -> (b s) d")
    ot = out.rearrange("b s d -> (b s) d")

    top = ExitStack()
    with top:
        def area():
            stack = ExitStack()

            def sb(name, shape, dt=F32):
                return stack.enter_context(nc.sbuf_tensor(name, shape, dt))
            return stack, sb

        def parts(stack, name, shape):
            hi = stack.enter_context(nc.sbuf_tensor(f"{name}_hi", shape, F32R))
            with nc.sbuf_tensor(f"{name}_in", shape, F32) as whole:
                pass
            return hi, stack.enter_context(nc.sbuf_tensor(f"{name}_lo", shape, F32R)), whole

        def sem(name):
            return top.enter_context(nc.semaphore(name))

        def sems(name, n):
            return [sem(f"{name}{i}") for i in range(n)]

        bank = [top.enter_context(nc.psum_tensor(f"bank{i}", [P, BANK], F32)) for i in range(8)]

        def const(name, shape, dt=F32):
            return top.enter_context(nc.sbuf_tensor(name, shape, dt))

        ident = const("ident", [P, P])
        ident_r = const("ident_r", [P, P], F32R)
        mask_r = const("mask_r", [P, REP, P], F32R)
        ones_r = const("ones_r", [P, P], F32R)
        neg_half = const("neg_half", [P, 1])
        tab = const("tab", [P, 2, 2, 2 * HD])
        nmax, rsum, rinv = const("nmax", [P, 4, REP]), const("rsum", [P, 4, REP]), const("rinv", [P, 4, REP])
        st1, mv1, rs1 = const("st1", [P, 2, 2, 6]), const("mv1", [P, 2, 2]), const("rs1", [P, 2, 2])
        b_raw = const("b_raw", [P, 2, KT])
        b_hl = const("b_hl", [P, 2, KT, 2], F32R)
        b_prod, b_part = const("b_prod", [P, KT]), const("b_part", [P, 1])
        ones = const("ones", [P, P])
        bA, cD = const("bA", [P, KT]), const("cD", [P, 1])
        u_bc = const("u_bc", [P, D])

        a1, sb = area()
        w_hi, w_lo, w_in = parts(a1, "w", [P, KT, QKV])
        x_st = sb("x_st", [P, 2, D])
        qT_hi, qT_lo = sb("qT_hi", [P, RB, P], F32R), sb("qT_lo", [P, RB, P], F32R)
        pick = [sb("pick0", [P, D], I32), sb("pick1", [P, D], I32)]
        raw = sb("raw", [P, ROPE])
        planes = sb("planes", [P, BITS, D // 32], I32)
        lut = sb("lut", [P, LEVELS])
        lut_x = sb("lut_x", [P, LEVELS // 2], I32)
        sb("pad_w", [P, 4 * KT * D - 2 * KT * QKV - 4 * D - 2 * RB * P - ROPE - BITS * D // 32 - LEVELS - LEVELS // 2])
        for i in range(2):
            sb(f"pad_q3_{i}", [P, REP, SEQ]), sb(f"pad_k3_{i}", [P, SEQ]), sb(f"pad_v_{i}", [P, 2, HD])
        rot_c, rot_s = sb("rot_c", [P, ROPE]), sb("rot_s", [P, ROPE])
        sb("pad_slots", [P, 2 * (REP * SEQ + SEQ + 2 * HD) - 2 * ROPE])
        xT_hi, xT_lo = sb("xT_hi", [P, 2, KT, P], F32R), sb("xT_lo", [P, 2, KT, P], F32R)
        turned = sb("turned", [P, ROPE])
        v_st = sb("v_st", [P, 2, KCOLS])
        bits = sb("bits", [P, BITS, D], I32)
        pick += [sb("pick2", [P, D], I32), sb("pick3", [P, D], I32)]
        a1.close()
        f_out = [pick[i][:, :].bitcast(F32R) for i in (2, 3)]

        a2, sb = area()
        wo_hi, wo_lo, wo_in = parts(a2, "wo", [P, KT, D])
        wq_hi, wq_lo, wq_in = parts(a2, "wq", [P, KT, D])
        q3, k3, vv = [], [], []
        for i in range(SLOTS):
            q3.append(sb(f"q3_{i}", [96, REP, SEQ], F32R))
            k3.append(sb(f"k3_{i}", [96, SEQ], F32R))
            vv.append(sb(f"vv_{i}", [P, 2, HD]))
        prob = sb("prob", [P, 4, BANK])
        probT = sb("probT", [P, 4, BANK])
        att = sb("att", [P, KT, SEQ])
        att_hi, att_lo = sb("att_hi", [P, KT, SEQ], F32R), sb("att_lo", [P, KT, SEQ], F32R)
        y1 = sb("y1", [P, 2, D])
        a2.close()

        a3, sb = area()
        m_hi, m_lo = sb("m_hi", [P, KT, D], F32R), sb("m_lo", [P, KT, D], F32R)
        a3_wk = ExitStack()
        for name, shape in (("pad_wq", [P, 2, KT, D]), ("pad_ctx", [P, GT, D])):
            a3_wk.enter_context(nc.sbuf_tensor(name, shape, F32))
        wk_hi, wk_lo, wk_in = parts(a3_wk, "wk", [P, 2, KT, P])
        a3_wk.close()

        cT_hi, cT_lo = sb("cT_hi", [P, KT, GROUP], F32R), sb("cT_lo", [P, KT, GROUP], F32R)
        k_hi, k_lo = sb("k_hi", [P, KT, GROUP], F32R), sb("k_lo", [P, KT, GROUP], F32R)
        ctx_st = sb("ctx_st", [P, 2, GT, D])
        x1_st = sb("x1_st", [P, GT, D])
        with nc.sbuf_tensor("b_rows", [P, 2, D], F32) as b_rows:
            pass
        x1T_hi, x1T_lo = sb("x1T_hi", [P, KT, P], F32R), sb("x1T_lo", [P, KT, P], F32R)
        d_hi, d_lo = sb("d_hi", [P, GROUP], F32R), sb("d_lo", [P, GROUP], F32R)
        cu, s_sum, s_key = sb("cu", [P, D]), sb("s_sum", [P, GT]), sb("s_key", [P, GT])
        pc, pcT = sb("pc", [P, 2, SEQ]), sb("pcT", [P, 2, 2, P])
        nm2, rs2, ri2 = sb("nm2", [P, GT, 2]), sb("rs2", [P, GT]), sb("ri2", [P, GT])
        st2, mv2, rv2 = sb("st2", [P, GT, 2, 6]), sb("mv2", [P, GT, 2]), sb("rv2", [P, GT, 2])
        a3.close()

        a5, sb = area()
        f_hi, f_lo = sb("f_hi", [P, KT, D], F32R), sb("f_lo", [P, KT, D], F32R)
        x2_st = sb("x2_st", [P, 2, D])
        x2b = sb("x2b", [P, 2, D])
        x2T_hi, x2T_lo = sb("x2T_hi", [P, 2, KT, P], F32R), sb("x2T_lo", [P, 2, KT, P], F32R)
        y3 = sb("y3", [P, 2, D])
        bias_bc = sb("bias_bc", [P, D])
        st3, mv3, rv3 = sb("st3", [P, 2, 2, 6]), sb("mv3", [P, 2, 2]), sb("rv3", [P, 2, 2])
        a5.close()

        consts_step, consts_done, tab_ld = sem("consts_step"), sem("consts_done"), sem("tab_ld")
        w_ld, x_ld = sems("w_ld", KT), sems("x_ld", 2)
        w_hi_ready, w_lo_ready = sem("w_hi_ready"), sem("w_lo_ready")
        xps_ready, xT_hi_ready, xT_lo_ready = sem("xps_ready"), sem("xT_hi_ready"), sem("xT_lo_ready")
        qkv_done, raw_ready, cos_done, sin_done, turned_ready = (
            sems("qkv_done", 3), sems("raw_ready", 3), sems("cos_done", 3), sems("sin_done", 3), sems("turned_ready", 3))
        qps_ready, qT_hi_ready, qT_lo_ready = sems("qps_ready", 3), sem("qT_hi_ready"), sem("qT_lo_ready")
        qhi_st, qlo_st, v_stored = sem("qhi_st"), sem("qlo_st"), sems("v_stored", 2)
        planes_ld, lut_ld, bits_ready, lutx_ready, pick_step = (
            sem("planes_ld"), sem("lut_ld"), sem("bits_ready"), sem("lutx_ready"), sem("pick_step"))
        fps_ready, f_hi_ready, f_lo_ready, f_stored = sem("fps_ready"), sem("f_hi_ready"), sem("f_lo_ready"), sem("f_stored")
        wo_ld, wo_hi_ready, wo_lo_ready = sem("wo_ld"), sem("wo_hi_ready"), sem("wo_lo_ready")
        wq_ld, wq_hi_ready, wq_lo_ready = sem("wq_ld"), sem("wq_hi_ready"), sem("wq_lo_ready")
        unit_ld, s_done, nmax_ready, exp_done, rinv_ready, prob_ready = (
            sems("unit_ld", SLOTS), sem("s_done"), sem("nmax_ready"), sem("exp_done"), sem("rinv_ready"), sem("prob_ready"))
        pT_done, pT_act, pT_dve, pv_done, att_ready, att_hi_ready, att_lo_ready = (
            sem("pT_done"), sem("pT_act"), sem("pT_dve"), sem("pv_done"), sem("att_ready"), sem("att_hi_ready"),
            sem("att_lo_ready"))
        wo_done, wo_pair, y1_part, y1_stats, y1_mv, y1_var, y1_rstd, y1_ready = (
            sem("wo_done"), sem("wo_pair"), sem("y1_part"), sem("y1_stats"), sem("y1_mv"), sem("y1_var"), sem("y1_rstd"), sem("y1_ready"))
        y1_ld, x1_stored = sems("y1_ld", 2), sems("x1_stored", 2)
        wk_ld, b_ld, wk_hi_ready, wk_lo_ready = sems("wk_ld", 2), sem("b_ld"), sem("wk_hi_ready"), sem("wk_lo_ready")
        bhi_ready, blo_ready, b_part_step, bA_done, bA_ready, b_spread, cD_ready = (
            sem("bhi_ready"), sem("blo_ready"), sem("b_part_step"), sem("bA_done"), sem("bA_ready"),
            sem("b_spread"), sem("cD_ready"))
        m_done, m_hi_ready, m_lo_ready, u_done, urow_ready, ubc_ready = (
            sem("m_done"), sem("m_hi_ready"), sem("m_lo_ready"), sem("u_done"), sem("urow_ready"), sem("ubc_ready"))
        ctx_ld, x1_ld = sems("ctx_ld", 2), sems("x1_ld", GT)
        cps_ready, cps_free, cT_hi_ready = sem("cps_ready"), sem("cps_free"), sem("cT_hi_ready")
        x1ps_ready, x1ps_free, x1T_hi_ready = sem("x1ps_ready"), sem("x1ps_free"), sem("x1T_hi_ready")
        acc_done, acc_free, k_hi_ready = sem("acc_done"), sem("acc_free"), sem("k_hi_ready")
        cu_ready, cu_free, s_ready, d_hi_ready, d_ready = (
            sem("cu_ready"), sem("cu_free"), sem("s_ready"), sem("d_hi_ready"), sem("d_ready"))
        s2_main, s2_done, nmax2_raw, nmax2_ready, exp2_done, rinv2_ready, p2T_done, p2T_ready = (
            sem("s2_main"), sem("s2_done"), sem("nmax2_raw"), sem("nmax2_ready"), sem("exp2_done"), sem("rinv2_ready"),
            sem("p2T_done"), sem("p2T_ready"))
        y2_stats, y2_mv, y2_var, y2_rstd, y2_ready, x2_stored = (
            sem("y2_stats"), sem("y2_mv"), sem("y2_var"), sem("y2_rstd"), sem("y2_ready"), sems("x2_stored", GT))
        f_ld, bias_ld, x2_ld = sem("f_ld"), sem("bias_ld"), sems("x2_ld", 2)
        x2ps_ready, x2T_hi_ready, x2T_lo_ready, x2b_ready, ffn_done = (
            sem("x2ps_ready"), sem("x2T_hi_ready"), sem("x2T_lo_ready"), sem("x2b_ready"), sem("ffn_done"))
        y3_part, y3_stats, y3_mv, y3_var, y3_rstd, y3_ready, out_stored = (
            sem("y3_part"), sem("y3_stats"), sem("y3_mv"), sem("y3_var"), sem("y3_rstd"), sem("y3_ready"),
            sems("out_stored", 2))

        CHUNK_BANK = (bank[0], bank[1], bank[2])
        XPS = (bank[3], bank[4])
        QPS = (bank[5], bank[6], bank[7])
        QBLK = ((0, 4), (4, 8), (8, 10))
        PIECE = (((0, 256, 0), (256, 512, 1)), ((512, 1024, 1),), ((1024, 1280, 1),))

        SUB = 3 * KVH
        LAG = 3
        PV_LAG = LAG + 2
        OUT_LAG = PV_LAG
        SBANK = (bank[0], bank[1], bank[2])
        TBANK = (bank[3], bank[4])
        OBANK = bank[5]
        WBANK = (bank[6], bank[7])
        WO_STEP = 2
        ADD_STEP = {12: (1, 0), 14: (1, 1), 20: (1, 2), 2: (2, 3)}
        RSTD_STEP = {14: (1, 0), 2: (2, 1)}
        NORM_STEP = {16: (1, 0), 4: (2, 1)}
        SPLIT_STEP = {22: (0, 0), 23: (0, 1), 1: (1, 2), 5: (1, 3)}
        LOW_STEP = {23: (0, 0), 0: (1, 1), 2: (1, 2), 6: (1, 3)}
        Q_TAIL_STEP, F_TAIL_STEP = 2, 8
        WO_STEPS = {14 + kt: kt for kt in range(KT)}
        WQ_STEP = 10

        def heads_of(pos):
            return (0, 1) if pos == 0 else (2, 3) if pos == 1 else (0, 1, 2, 3)

        def probT_used(b, k):
            return 2 * (KVH * b + k // 3) - (2 if k % 3 == 0 else 1)

        def keys_of(pos):
            return 2 * P if pos < 2 else P

        CPS, X1PS, ACC, SPS = (bank[0], bank[1]), (bank[2], bank[3]), (bank[4], bank[5]), (bank[6], bank[7])

        def key_use(it):
            return it - 1 if it else ACC_USES - 3

        def att_use(t, half, last):
            return KT - 1 + 2 * t + half + (1 if t == GT - 1 and not last else 0)

        def use_of(g, i):
            return ACC_USES * g + i + 1

        def acc_bank(a, i):
            return ACC[use_of(a, i) % 2]

        X2PS, YPS = (bank[2], bank[3]), ((bank[0], bank[1]), (bank[4], bank[5]))

        block = top.enter_context(nc.Block())

        def wait(eng, s, value):
            if not (isinstance(value, int) and value <= 0):
                eng.wait_ge(s, value)

        def wait_alone(eng, s, value):
            wait(eng, s, value)
            eng.nop(nofuse=True)

        @block.sync
        def _(sp):
            def load_x(n, slot):
                sp.dma_start(x_st[:, slot, :], xt[bass.ds(n * P, P), :]).then_inc(x_ld[slot], 16)

            def load_planes(b):
                sp.dma_start(planes[:, :, :], qweight[0:BITS, bass.ds(b * P, P), :].rearrange("q o w -> o q w"))\
                  .then_inc(planes_ld, 16)

            def load_lut(b):
                sp.dma_start(lut[:, :], lut4[bass.ds(b * P, P), :]).then_inc(lut_ld, 16)

            load_x(0, 0)
            for kt in range(KT):
                rows = w_qkv[kt * P:(kt + 1) * P, :]
                sp.dma_start(w_in[:, kt, KCOLS:ROPE], rows[:, 0:HEADS * HD]).then_inc(w_ld[kt], 16)
                ends = w_in[:, kt, :].rearrange("p (s c) -> p s c", c=KCOLS)[:, 0:QKV // KCOLS:QKV // KCOLS - 1, :]
                sp.dma_start(ends, rows[:, HEADS * HD:QKV].rearrange("p (s c) -> p s c", c=KCOLS))\
                  .then_inc(w_ld[kt], 16)
                if kt == 1:
                    load_x(1, 1)
            sp.dma_start(tab[:, :, :, :], rope.rearrange("(j p) t c -> p j t c", p=P)).then_inc(tab_ld, 16)
            load_planes(0)
            load_lut(0)
            for i, v in enumerate((bq, bk)):
                with nc.allow_non_contiguous_dma(reason="two short vectors, once"):
                    sp.dma_start(b_raw[:, i, :], v.rearrange("(t p) -> p t", p=P)).then_inc(b_ld, 16)
            sp.wait_ge(xps_ready, 2)
            load_x(2, 0)

            def store_q(n):
                for i, (t, ready, count, stored) in enumerate(((qT_hi, qT_hi_ready, 3, qhi_st), (qT_lo, qT_lo_ready, 3, qlo_st))):
                    wait_alone(sp, ready, count * n + count)
                    sp.dma_start(qk_scr[i].rearrange("(c p) s -> p c s", p=P)[:, :, bass.ds(n * P, P)],
                                 t[:, :, :].bitcast(F32)).then_inc(stored, 16)

            def store_f(b):
                sp.wait_ge(f_lo_ready, 2 * b + 2)
                for i in range(2):
                    sp.dma_start(f_scr[i].rearrange("(k p) o -> p k o", p=P)[:, :, bass.ds(b * P, P)],
                                 f_out[i].bitcast(F32).rearrange("p (k o) -> p k o", o=P)).then_inc(f_stored, 16)

            def stage1_batch(b, ahead, first, last):
                for j in range(2):
                    n = 2 * b + j
                    if not (first and j == 0):
                        store_q(n - 1)
                    if j == 0 and not first:
                        store_f(b - 1)
                        sp.wait_ge(pick_step, PICKS * b)
                        load_lut(b)
                    if j == 1 and not last:
                        sp.wait_ge(bits_ready, b + 1)
                        load_planes(b + 1)
                    if ahead[j]:
                        sp.wait_ge(xps_ready, 2 * n + 4)
                        load_x(n + 3, 1 - j)
                    sp.wait_ge(raw_ready[2], n + 1)
                    sp.dma_start(v_scr[bass.ds(n * P, P), :], v_st[:, j, :]).then_inc(v_stored[j], 16)

            def load_unit(b, unit, free=True):
                slot, s = unit % SLOTS, bass.ds(b * SEQ, SEQ)
                if free:
                    sp.wait_ge(pv_done, 2 * (KVH * b + unit - SLOTS + 1))
                for part, (qp, kp) in enumerate(((0, 0), (0, 1), (1, 0))):
                    rows = slice(HD * part, HD * (part + 1))
                    sp.dma_start(q3[slot][rows, :, :].bitcast(F32),
                                 qk_scr[qp, KCOLS + P * unit:KCOLS + P * (unit + 1), s].rearrange("(h d) s -> d h s", d=HD))\
                      .then_inc(unit_ld[slot], 16)
                    sp.dma_start(k3[slot][rows, :].bitcast(F32), qk_scr[kp, HD * unit:HD * (unit + 1), s])\
                      .then_inc(unit_ld[slot], 16)
                sp.dma_start(vv[slot][:, :, :], v_scr[s, HD * unit:HD * (unit + 1)].rearrange("(t p) c -> p t c", p=P))\
                  .then_inc(unit_ld[slot], 16)

            stage1_batch(0, (True, True), True, False)
            with sp.Fori(1, BATCH - 2) as b:
                stage1_batch(b, (True, True), False, False)
            stage1_batch(BATCH - 2, (True, False), False, False)
            sp.wait_ge(qhi_st, 16 * (TILES - 3))
            sp.wait_ge(qlo_st, 16 * (TILES - 3))
            sp.wait_ge(v_stored[0], 16 * (BATCH - 1))
            sp.wait_ge(v_stored[1], 16 * (BATCH - 1))
            for unit in range(2):
                load_unit(0, unit, False)
            stage1_batch(BATCH - 1, (False, False), False, True)

            sp.wait_ge(turned_ready[2], TILES)
            for unit in range(2, SLOTS):
                load_unit(0, unit, False)
            store_q(TILES - 1)

            def load_wo(kts):
                for kt in kts:
                    sp.dma_start(wo_in[:, kt, :], w_o[kt * P:(kt + 1) * P, :]).then_inc(wo_ld, 16)

            load_wo(range(0, 3))
            def load_y1(b, st):
                if not isinstance(b, int) or b:
                    sp.wait_ge(x1_stored[st], 16 * b)
                sp.dma_start(y1[:, st, :], xt[bass.ds(b * SEQ + st * P, P), :]).then_inc(y1_ld[st], 16)

            def store_x1(b, st):
                sp.wait_ge(y1_ready, 2 * b + st + 1)
                sp.dma_start(x1_scr[bass.ds(b * SEQ + st * P, P), :], y1[:, st, :]).then_inc(x1_stored[st], 16)

            load_unit(0, 4)
            load_wo(range(3, 6))
            store_f(BATCH - 1)
            load_unit(0, 5)
            load_wo(range(6, KT))
            sp.wait_ge(f_stored, 32 * BATCH)
            sp.wait_ge(qhi_st, 16 * TILES)
            sp.wait_ge(qlo_st, 16 * TILES)
            for st in range(2):
                sp.wait_ge(v_stored[st], 16 * BATCH)
                load_y1(0, st)
            load_unit(0, 6)
            load_unit(0, 7)
            for dt in range(KT):
                sp.dma_start(wq_in[:, dt, :], wq[dt * P:(dt + 1) * P, :]).then_inc(wq_ld, 16)
                if dt % 4 == 3:
                    load_unit(1, dt // 4)

            def stage2_batch(b, age, last):
                load_unit(b, 2)
                load_unit(b, 3)
                if age >= 2:
                    store_x1(b - 2, 1)
                load_unit(b, 4)
                if age >= 2:
                    load_y1(b - 1, 1)
                for unit in range(5, KVH):
                    load_unit(b, unit)
                store_x1(b - 1, 0)
                if not last:
                    load_unit(b + 1, 0)
                load_y1(b, 0)
                if not last:
                    load_unit(b + 1, 1)
            stage2_batch(1, 1, False)
            with sp.Fori(2, BATCH - 1) as b:
                stage2_batch(b, 2, False)
            stage2_batch(BATCH - 1, 2, True)

            def load_wk(m):
                if m >= 2:
                    sp.wait_ge(u_done, m - 1)
                    sp.wait_ge(m_done, 2 * (m - 1))
                sp.dma_start(wk_in[:, m % 2, :, :], wk[:, m * P:(m + 1) * P].rearrange("(t p) c -> p t c", p=P))\
                  .then_inc(wk_ld[m % 2], 16)

            def load_ctx(g, a):
                for t in range(GT):
                    sp.dma_start(ctx_st[:, a, t, :], cx[bass.ds(g * GROUP + t * P, P), :]).then_inc(ctx_ld[a], 16)

            def load_x1(g, t):
                if not isinstance(g, int) or g:
                    sp.wait_ge(x2_stored[t], 16 * g)
                sp.dma_start(x1_st[:, t, :], x1_scr[bass.ds(g * GROUP + t * P, P), :]).then_inc(x1_ld[t], 16)

            def store_x2(g, t):
                sp.wait_ge(y2_ready, GT * g + t + 1)
                sp.dma_start(x2_scr[bass.ds(g * GROUP + t * P, P), :], x1_st[:, t, :]).then_inc(x2_stored[t], 16)

            sp.wait_ge(pv_done, 2 * KVH * BATCH)
            load_wk(0)
            load_wk(1)
            load_ctx(0, 0)
            store_x1(BATCH - 2, 1)
            load_y1(BATCH - 1, 1)
            for st in range(2):
                store_x1(BATCH - 1, st)
            for st in range(2):
                sp.wait_ge(x1_stored[st], 16 * BATCH)
            for t in range(GT):
                load_x1(0, t)
            for m in range(2, KT):
                load_wk(m)
            sp.wait_ge(m_done, 2 * KT)
            load_ctx(1, 1)

            def stage4_group(g, a, last):
                if last:
                    sp.wait_ge(acc_done, use_of(g, key_use(KT - 1)) + 1)
                    for n in range(2):
                        sp.dma_start(x2_st[:, n, :], x2_scr[n * P:(n + 1) * P, :]).then_inc(x2_ld[n], 16)
                    for kt in range(KT):
                        for i, f in enumerate((f_hi, f_lo)):
                            sp.dma_start(f[:, kt, :].bitcast(F32), f_scr[i, kt * P:(kt + 1) * P, :]).then_inc(f_ld, 16)
                for t in range(GT):
                    store_x2(g, t)
                    if last and t == 1:
                        sp.wait_ge(s2_done, GT * GROUPS)
                        sp.dma_start(bias_bc[:, :], bias.rearrange("(a n) -> a n", a=1).to_broadcast([P, D])).then_inc(bias_ld, 16)
                    if t and not last:
                        load_x1(g + 1, t - 1)
                if not last:
                    load_x1(g + 1, GT - 1)

            def next_ctx(g, a):
                sp.wait_ge(acc_done, use_of(g, att_use(GT - 1, 1, False)) + 1)
                load_ctx(g + 2, a)

            with sp.Fori(0, GROUPS // 2 - 1) as g2:
                for a in range(2):
                    stage4_group(2 * g2 + a, a, False)
                    next_ctx(2 * g2 + a, a)
            stage4_group(GROUPS - 2, 0, False)
            stage4_group(GROUPS - 1, 1, True)

            for t in range(GT):
                sp.wait_ge(x2_stored[t], 16 * GROUPS)

            def stage5_batch(b, last):
                for j in range(2):
                    n = 2 * b + j
                    if not last:
                        sp.wait_ge(x2b_ready, n + 1)
                        sp.wait_ge(x2ps_ready, 2 * n + 2)
                        sp.dma_start(x2_st[:, j, :], x2_scr[bass.ds((n + 2) * P, P), :]).then_inc(x2_ld[j], 16)
                    sp.wait_ge(y3_ready, n + 1)
                    sp.dma_start(ot[bass.ds(n * P, P), :], y3[:, j, :]).then_inc(out_stored[j], 16)
            with sp.Fori(0, BATCH - 1) as b:
                stage5_batch(b, False)
            stage5_batch(BATCH - 1, True)
            sp.wait_ge(out_stored[0], 16 * BATCH)
            sp.wait_ge(out_stored[1], 16 * BATCH)

        @block.tensor
        def _(pe):
            def product(o, l_hi, l_lo, r_hi, r_lo, first, last):
                nc.tensor.matmul(o, l_hi, r_hi, start=first, stop=False)
                nc.tensor.matmul(o, l_hi, r_lo, start=False, stop=False)
                return nc.tensor.matmul(o, l_lo, r_hi, start=False, stop=last)

            def turn(src, banks, ready):
                for h in range(2):
                    for i in range(4):
                        kt = 4 * h + i
                        mm = nc.tensor.transpose(banks[h][:, i * P:(i + 1) * P], src[:, kt * P:(kt + 1) * P], ident[:, :])
                    mm.then_inc(ready, 1)

            def turn_q(n, g):
                lo, hi = QBLK[g]
                pe.wait_ge(turned_ready[g], n + 1)
                wait(pe, qT_lo_ready, 3 * n + g - 2)
                for i in range(lo, hi):
                    mm = nc.tensor.transpose(QPS[g][:, (i - lo) * P:(i - lo + 1) * P], turned[:, i * P:(i + 1) * P], ident[:, :])
                mm.then_inc(qps_ready[g], 1)

            def turn_f(b, banks=XPS):
                pe.wait_ge(pick_step, PICKS * b + PICKS)
                turn(pick[0][:, :].bitcast(F32), banks, fps_ready)

            def stage1_batch(b, first, last):
                for j in range(2):
                    n = 2 * b + j

                    def qkv(c, kt):
                        return product(CHUNK_BANK[c][:, :], xT_hi[:, j, kt, :], xT_lo[:, j, kt, :],
                                       w_hi[:, kt, c * BANK:(c + 1) * BANK], w_lo[:, kt, c * BANK:(c + 1) * BANK],
                                       kt == 0, kt == KT - 1)

                    def turn_x():
                        pe.wait_ge(x_ld[1 - j], 16 * b + 16 * (j + 1))
                        if j == 0 and not first:
                            pe.wait_ge(f_lo_ready, 2 * b)
                        turn(x_st[:, 1 - j, :], XPS, xps_ready)

                    pe.wait_ge(xT_lo_ready, n + 1)
                    if first and j == 0:
                        for kt in range(KT):
                            pe.wait_ge(w_lo_ready, kt + 1)
                            for c in range(3):
                                mm = qkv(c, kt)
                                if kt == KT - 1:
                                    mm.then_inc(qkv_done[c], 1)
                            if kt == 5:
                                turn_x()
                        continue
                    for c in range(3):
                        wait(pe, raw_ready[c], n)
                        for kt in range(KT):
                            mm = qkv(c, kt)
                        mm.then_inc(qkv_done[c], 1)
                        if c == 0:
                            for g in range(3) if first else (2,):
                                turn_q(n - 1, g)
                            if j == 0:
                                turn_f(b - 1)
                        elif c == 1:
                            turn_q(n, 0)
                            if not (last and j == 1):
                                turn_x()
                        else:
                            turn_q(n, 1)

            pe.wait_ge(consts_done, 1)
            pe.wait_ge(x_ld[0], 16)
            turn(x_st[:, 0, :], XPS, xps_ready)
            stage1_batch(0, True, False)
            with pe.Fori(1, BATCH - 1) as b:
                stage1_batch(b, False, False)
            stage1_batch(BATCH - 1, False, True)

            def scores(b, k):
                u, pos, unit = SUB * b + k, k % 3, k // 3
                slot, o = unit % SLOTS, SBANK[pos]
                if pos == 0:
                    pe.wait_ge(unit_ld[slot], 7 * 16 * (KVH // SLOTS * b + unit // SLOTS + 1))
                wait(pe, exp_done, u - 2)
                if isinstance(u, int) and u == 2:
                    pe.wait_ge(raw_ready[2], TILES)
                hs, keys = heads_of(pos), keys_of(pos)
                t0 = P if pos < 2 else 0
                for i, h in enumerate(hs):
                    nc.tensor.matmul(o[:, i * keys:(i + 1) * keys], q3[slot][:, h, t0:t0 + P],
                                     k3[slot][:, 0:keys], start=i == 0, stop=False, skip_group_check=True)
                diag = o[:, 0:len(hs) * keys].rearrange("p (h t) -> p h t", t=keys)[:, :, keys - P:keys]
                nc.tensor.matmul(diag, ident_r[:, :], mask_r[:, 0:len(hs), :], start=False, stop=True,
                                 skip_group_check=True).then_inc(s_done, 1)

            def turn_probs(b, k):
                u, pos = SUB * b + k, k % 3
                pe.wait_ge(prob_ready, u + 1)
                taken(b, k - 2)
                tb = TBANK[k % 2]
                blocks = [(t, i) for t in range(keys_of(pos) // P) for i in range(len(heads_of(pos)))]
                for at, (t, i) in enumerate(blocks):
                    c = i * keys_of(pos) + t * P
                    mm = nc.tensor.transpose(tb[:, at * P:(at + 1) * P], prob[:, k % 4, c:c + P], ident[:, :])
                mm.then_inc(pT_done, 1)

            def taken(b, k):
                if isinstance(b, int) and SUB * b + k < 0:
                    return
                unit, pos = KVH * b + k // 3, k % 3
                if pos == 1:
                    pe.wait_ge(pT_dve, unit + 1)
                else:
                    pe.wait_ge(pT_act, 2 * unit + (1 if pos == 0 else 2))

            def weighted(b, k):
                pos, unit = k % 3, k // 3
                if pos == 0:
                    return
                taken(b, k - 1)
                taken(b, k)
                v = vv[unit % SLOTS]
                if pos == 1:
                    wait(pe, att_ready, KVH * b + unit)
                    for t in range(2):
                        for h in range(REP):
                            src = probT[:, (k - 1 + h // 2) % 4, (2 * t + h % 2) * P:(2 * t + h % 2 + 1) * P]
                            mm = nc.tensor.matmul(OBANK[HD * h:HD * (h + 1), P:2 * P], v[:, t, :], src,
                                                  start=t == 0, stop=t == 1, skip_group_check=True)
                else:
                    for h in range(REP):
                        mm = nc.tensor.matmul(OBANK[HD * h:HD * (h + 1), 0:P], v[:, 0, :],
                                              probT[:, k % 4, h * P:(h + 1) * P], start=True, stop=True,
                                              skip_group_check=True)
                mm.then_inc(pv_done, 1)

            WO = [(g, kt, ps) for kts in (range(KT - 2), range(KT - 2, KT)) for g in (0, 1) for kt in kts for ps in range(3)]
            WO += [(g, kt, ps) for g in (2, 3) for kt in range(KT) for ps in range(3)]

            def project(b, part):
                for g, kt, ps in part:
                    st, half = g // 2, g % 2
                    o = WBANK[g % 2]
                    if kt == 0 and ps == 0:
                        wait(pe, y1_part, 4 * b + g - 1)
                    if g == 0 and kt % 2 == 0 and ps == 0:
                        pe.wait_ge(att_lo_ready, 4 * b + kt // 2 + 1)
                    if g == 0 and ps == 0:
                        pe.wait_ge(wo_lo_ready, kt + 1)
                    lt = att_lo if ps == 2 else att_hi
                    rt = wo_lo if ps == 1 else wo_hi
                    mm = nc.tensor.matmul(o[:, :], lt[:, kt, st * P:(st + 1) * P], rt[:, kt, half * BANK:(half + 1) * BANK],
                                          start=kt == 0 and ps == 0, stop=kt == KT - 1 and ps == 2)
                    if kt == KT - 1 and ps == 2:
                        mm.then_inc(wo_done, 1)
                    elif g == 3 and kt % 2 and ps == 2:
                        mm.then_inc(wo_pair, 1)

            def project_step(b, k, age):
                i = k - WO_STEP
                part = WO[len(WO) * (i % SUB) // SUB:len(WO) * (i % SUB + 1) // SUB]
                if i >= 0 and age >= 1:
                    project(b - 1, part)
                if i < 0 and age >= 2:
                    project(b - 2, part)

            def stage2_batch(b, age):
                for k in range(SUB):
                    scores(b, k)
                    project_step(b, k, age)
                    if age == 0 and k == Q_TAIL_STEP:
                        turn_q(TILES - 1, 2)
                    if age == 0 and k == F_TAIL_STEP:
                        pe.wait_ge(qT_lo_ready, 3 * TILES)
                        turn_f(BATCH - 1, WBANK)
                    if age or k >= PV_LAG:
                        late(b, k - PV_LAG, weighted)
                    if age or k >= LAG:
                        late(b, k - LAG, turn_probs)

            def late(b, k, what):
                what(b - 1, k + SUB) if k < 0 else what(b, k)

            stage2_batch(0, 0)
            stage2_batch(1, 1)
            with pe.Fori(2, BATCH) as b:
                stage2_batch(b, 2)
            for k in range(PV_LAG):
                if k < LAG:
                    late(BATCH, k - LAG, turn_probs)
                late(BATCH, k - PV_LAG, weighted)
                if k < WO_STEP:
                    project_step(BATCH, k, 2)
            project(BATCH - 1, WO)

            pe.wait_ge(b_part_step, 2)
            pe.wait_ge(att_ready, KVH * BATCH)
            nc.tensor.matmul(OBANK[:, 0:1], ones[:, :], b_part[:, :], start=True, stop=True).then_inc(b_spread, 1)

            def fold(m, slot):
                pe.wait_ge(wk_lo_ready, m + 1)
                for half in range(2):
                    wait(pe, m_lo_ready, 2 * m + half - 3)
                    for dt in range(KT):
                        mm = product(bank[2 * slot + half][:, :], wk_hi[:, slot, dt, :], wk_lo[:, slot, dt, :],
                                     wq_hi[:, dt, half * BANK:(half + 1) * BANK],
                                     wq_lo[:, dt, half * BANK:(half + 1) * BANK], dt == 0, dt == KT - 1)
                    mm.then_inc(m_done, 1)

            def u_row(m, slot):
                pe.wait_ge(wk_lo_ready, m + 1)
                wait(pe, urow_ready, m)
                for dt in range(KT):
                    nc.tensor.matmul(bank[6][0:2, 0:P], b_hl[:, 0, dt, :], wk_hi[:, slot, dt, :], start=dt == 0, stop=False)
                    mm = nc.tensor.matmul(bank[6][0:2, 0:P], b_hl[:, 0, dt, :], wk_lo[:, slot, dt, :], start=False,
                                          stop=dt == KT - 1)
                mm.then_inc(u_done, 1)

            pe.wait_ge(blo_ready, 1)
            pe.wait_ge(wq_lo_ready, KT)
            fold(0, 0)
            pe.wait_ge(y1_part, 4 * BATCH)
            u_row(0, 0)
            for half, o in enumerate((bank[7], bank[4])):
                for dt in range(KT):
                    cols = slice(half * BANK, (half + 1) * BANK)
                    nc.tensor.matmul(o[0:2, :], b_hl[:, 1, dt, :], wq_hi[:, dt, cols], start=dt == 0, stop=False)
                    mm = nc.tensor.matmul(o[0:2, :], b_hl[:, 1, dt, :], wq_lo[:, dt, cols], start=False, stop=dt == KT - 1)
                mm.then_inc(bA_done, 1)
            u_row(1, 1)
            fold(1, 1)
            with pe.Fori(1, KT // 2) as m2:
                for slot in range(2):
                    u_row(2 * m2 + slot, slot)
                    fold(2 * m2 + slot, slot)
            pe.wait_ge(bA_ready, 2)
            pe.wait_ge(urow_ready, KT)
            pe.wait_ge(cD_ready, 1)
            for it in range(KT):
                mm = nc.tensor.matmul(OBANK[:, it:it + 1], b_rows[0:2, 1, it * P:(it + 1) * P], ones[0:2, 0:1], start=True,
                                      stop=True)
            mm.then_inc(b_spread, 1)
            for half in range(2):
                nc.tensor.matmul(WBANK[half][:, :], ones[0:2, :], b_rows[0:2, 0, half * BANK:(half + 1) * BANK], start=True,
                                 stop=True).then_inc(b_spread, 1)

            def turn_ctx(g, a, kt):
                if kt == 0:
                    pe.wait_ge(ctx_ld[a], GT * 8 * (g - a + 2))
                pe.wait_ge(cps_free, KT * g + kt + 1)
                for t in range(GT):
                    mm = nc.tensor.transpose(CPS[kt % 2][:, t * P:(t + 1) * P], ctx_st[:, a, t, kt * P:(kt + 1) * P], ident[:, :])
                mm.then_inc(cps_ready, 1)

            def turn_x1(g, t):
                pe.wait_ge(x1_ld[t], 16 * g + 16)
                for h in range(2):
                    pe.wait_ge(x1ps_free, 2 * (GT * g + t) + h + 1)
                    for i in range(4):
                        kt = 4 * h + i
                        mm = nc.tensor.transpose(X1PS[h][:, i * P:(i + 1) * P], x1_st[:, t, kt * P:(kt + 1) * P], ident[:, :])
                    mm.then_inc(x1ps_ready, 1)

            def acc_wait(g, i):
                pe.wait_ge(acc_free, use_of(g, i) + 1)

            def keys(o, it, split=None):
                for kt in range(KT):
                    if split is not None:
                        pe.wait_ge(cps_free, split + kt + 3)
                    mm = product(o, m_hi[:, kt, it * P:(it + 1) * P], m_lo[:, kt, it * P:(it + 1) * P],
                                 cT_hi[:, kt, :], cT_lo[:, kt, :], kt == 0, kt == KT - 1)
                mm.then_inc(acc_done, 1)

            def cross_main(g, t):
                e = t // 2
                pe.wait_ge(x1ps_free, 2 * (GT * g + t) + 4)
                o, s = SPS[t % 2][:, 0:SEQ], slice(e * SEQ, (e + 1) * SEQ)
                for kt in range(KT):
                    if t == 0 and kt in (0, KT - 2, KT - 1):
                        pe.wait_ge(acc_free, use_of(g, key_use(max(kt, KT - 3))) + 3)
                    mm = product(o, x1T_hi[:, kt, :], x1T_lo[:, kt, :], k_hi[:, kt, s], k_lo[:, kt, s], kt == 0, False)
                mm.then_inc(s2_main, 1)

            def cross_sum(g, t):
                e = t // 2
                o, s = SPS[t % 2][:, 0:SEQ], slice(e * SEQ, (e + 1) * SEQ)
                if t == 0:
                    pe.wait_ge(d_ready, GT * g + GT)
                nc.tensor.matmul(o, ones_r[:, :], d_hi[:, s], start=False, stop=False)
                nc.tensor.matmul(o, ones_r[:, :], d_lo[:, s], start=False, stop=True).then_inc(s2_done, 1)

            def turn_probs2(g, t):
                pe.wait_ge(exp2_done, GT * g + t + 1)
                for i in range(2):
                    mm = nc.tensor.transpose(SPS[t % 2][:, SEQ + i * P:SEQ + (i + 1) * P], pc[:, t % 2, i * P:(i + 1) * P],
                                             ident[:, :])
                mm.then_inc(p2T_done, 1)

            def attended(g, a, t, last):
                e = t // 2
                pe.wait_ge(p2T_ready, GT * g + t + 1)
                for half in range(2):
                    i = att_use(t, half, last)
                    acc_wait(g, i)
                    for kb in range(2):
                        mm = nc.tensor.matmul(acc_bank(a, i)[:, :], pcT[:, t % 2, kb, :],
                                              ctx_st[:, a, 2 * e + kb, half * BANK:(half + 1) * BANK], start=kb == 0, stop=kb == 1)
                    mm.then_inc(acc_done, 1)

            def turn_first_x2():
                pe.wait_ge(x2_ld[0], 16)
                turn(x2_st[:, 0, :], X2PS, x2ps_ready)

            def cross_group(g, a, last):
                def ahead(kt):
                    if not last:
                        turn_ctx(g + 1, 1 - a, kt)

                for it in range(1, KT):
                    acc_wait(g, key_use(it))
                    keys(acc_bank(a, key_use(it))[:, :], it)
                    if it == 5:
                        turn_x1(g, 0)
                turn_x1(g, 1)
                cross_main(g, 0)
                ahead(0)
                turn_x1(g, 2)
                cross_sum(g, 0)
                cross_main(g, 1)
                turn_probs2(g, 0)
                cross_sum(g, 1)
                ahead(1)
                attended(g, a, 0, last)
                turn_probs2(g, 1)
                ahead(2)
                cross_main(g, 2)
                cross_sum(g, 2)
                turn_x1(g, 3)
                ahead(3)
                attended(g, a, 1, last)
                turn_probs2(g, 2)
                ahead(4)
                cross_main(g, 3)
                cross_sum(g, 3)
                ahead(5)
                attended(g, a, 2, last)
                if last:
                    turn_first_x2()
                ahead(6)
                ahead(7)
                if not last:
                    acc_wait(g, key_use(0))
                    keys(acc_bank(a, key_use(0))[:, :], 0, KT * (g + 1))
                turn_probs2(g, 3)
                attended(g, a, 3, last)

            pe.wait_ge(m_lo_ready, 2 * KT - 2)
            for kt in range(KT):
                turn_ctx(0, 0, kt)
            pe.wait_ge(m_lo_ready, 2 * KT)
            pe.wait_ge(ubc_ready, 2)
            pe.wait_ge(bA_ready, 3)
            keys(ACC[0][:, :], 0, 0)
            with pe.Fori(0, GROUPS // 2 - 1) as g2:
                cross_group(2 * g2, 0, False)
                cross_group(2 * g2 + 1, 1, False)
            cross_group(GROUPS - 2, 0, False)
            cross_group(GROUPS - 1, 1, True)

            pe.wait_ge(f_ld, 32 * KT)

            def ffn_batch(b, last):
                for j in range(2):
                    n = 2 * b + j
                    pe.wait_ge(x2T_lo_ready, n + 1)
                    for half in range(2):
                        wait(pe, y3_part, 2 * n - 2)
                        for kt in range(KT):
                            mm = product(YPS[j][half][:, :], x2T_hi[:, j, kt, :], x2T_lo[:, j, kt, :],
                                         f_hi[:, kt, half * BANK:(half + 1) * BANK],
                                         f_lo[:, kt, half * BANK:(half + 1) * BANK], kt == 0, kt == KT - 1)
                        mm.then_inc(ffn_done, 1)
                        if half == 0 and not (last and j == 1):
                            pe.wait_ge(x2_ld[1 - j], 16 * b + 16 * (j + 1))
                            turn(x2_st[:, 1 - j, :], X2PS, x2ps_ready)
            ffn_batch(0, False)
            with pe.Fori(1, BATCH - 1) as b:
                ffn_batch(b, False)
            ffn_batch(BATCH - 1, True)

        @block.scalar
        def _(act):
            nc.scalar.preload_act_table(ACT.Exp)

            def copy(o, i):
                return nc.scalar.activation(o, i, ACT.Copy)

            def tile_high(banks, dst, first, ready, done):
                for h in range(2):
                    act.wait_ge(ready, first + h + 1)
                    copy(dst[:, 4 * h:4 * h + 4, :].rearrange("p k s -> p (k s)"), banks[h][:, :]).then_inc(done, 1)

            def x_high(n, slot):
                tile_high(XPS, xT_hi[:, slot, :, :], 2 * n, xps_ready, xT_hi_ready)

            def q_high(n, g):
                lo, hi = QBLK[g]
                act.wait_ge(qps_ready[g], n + 1)
                if g == 0:
                    wait(act, qhi_st, 16 * n)
                copy(qT_hi[:, lo:hi, :].rearrange("p c s -> p (c s)"), QPS[g][:, 0:(hi - lo) * P]).then_inc(qT_hi_ready, 1)

            def f_high(b, banks=XPS):
                for h in range(2):
                    act.wait_ge(fps_ready, 2 * b + h + 1)
                    copy(f_out[0][:, h * BANK:(h + 1) * BANK], banks[h][:, :]).then_inc(f_hi_ready, 1)

            def stage1_batch(b, first, last):
                for j in range(2):
                    n = 2 * b + j
                    for c in range(3):
                        act.wait_ge(qkv_done[c], n + 1)
                        wait(act, cos_done[c], n)
                        wait(act, sin_done[c], n)
                        lo, hi = c * BANK, min((c + 1) * BANK, ROPE)
                        mm = copy(raw[:, lo:hi], CHUNK_BANK[c][:, 0:hi - lo])
                        if c == 2:
                            wait(act, v_stored[j], 16 * b)
                            mm = copy(v_st[:, j, :], CHUNK_BANK[c][:, hi - lo:BANK])
                        mm.then_inc(raw_ready[c], 1)
                        if first and j == 0:
                            continue
                        if c == 0:
                            for g in range(3) if first else (2,):
                                q_high(n - 1, g)
                            if j == 0:
                                f_high(b - 1)
                        elif c == 1:
                            q_high(n, 0)
                            if not (last and j == 1):
                                x_high(n + 1, 1 - j)
                        else:
                            q_high(n, 1)

            x_high(0, 0)
            for kt in range(KT):
                act.wait_ge(w_ld[kt], 32)
                copy(w_hi[:, kt, :], w_in[:, kt, :]).then_inc(w_hi_ready, 1)
            x_high(1, 1)
            stage1_batch(0, True, False)
            with act.Fori(1, BATCH - 1) as b:
                stage1_batch(b, False, False)
            stage1_batch(BATCH - 1, False, True)

            def exponent(b, k):
                u, pos = SUB * b + k, k % 3
                act.wait_ge(nmax_ready, u + 1)
                wait(act, pT_done, u - 3)
                wait(act, rinv_ready, u - 3)
                keys, n = keys_of(pos), len(heads_of(pos))
                for i in range(n):
                    mm = nc.scalar.activation(prob[:, k % 4, i * keys:(i + 1) * keys], SBANK[pos][:, i * keys:(i + 1) * keys],
                                              ACT.Exp, bias=nmax[:, k % 4, i:i + 1], accum_out=rsum[:, k % 4, i:i + 1])
                mm.then_inc(exp_done, 1)

            def probs_out(b, k):
                u, pos = SUB * b + k, k % 3
                if pos == 1:
                    return
                act.wait_ge(pT_done, u + 1)
                wait(act, pv_done, probT_used(b, k))
                copy(probT[:, k % 4, :], TBANK[k % 2][:, :]).then_inc(pT_act, 1)

            def att_high(b, pair):
                wait(act, att_ready, KVH * b + 2 * pair + 2)
                if pair < 3:
                    wait(act, wo_pair, 3 * b + pair - 2)
                else:
                    wait(act, wo_done, 4 * b)
                copy(att_hi[:, 2 * pair:2 * pair + 2, :].rearrange("p k s -> p (k s)"),
                     att[:, 2 * pair:2 * pair + 2, :].rearrange("p k s -> p (k s)")).then_inc(att_hi_ready, 1)

            def late(b, k, what):
                what(b - 1, k + SUB) if k < 0 else what(b, k)

            def wq_high(dt):
                one = lambda w: w[:, bass.ds(dt, 1), :]
                copy(one(wq_hi), one(wq_in)).then_inc(wq_hi_ready, 1)

            def stage2_batch(b, age):
                for k in range(SUB):
                    if age == 0:
                        if k >= LAG:
                            probs_out(b, k - LAG)
                        exponent(b, k)
                    else:
                        exponent(b, k)
                        late(b, k - LAG, probs_out)
                    if k in SPLIT_STEP and SPLIT_STEP[k][0] <= age:
                        att_high(b - SPLIT_STEP[k][0], SPLIT_STEP[k][1])
                    if age == 0 and k == Q_TAIL_STEP:
                        q_high(TILES - 1, 2)
                    if age == 0 and k == F_TAIL_STEP:
                        f_high(BATCH - 1, WBANK)
                    if age == 0 and k in WO_STEPS:
                        kt = WO_STEPS[k]
                        act.wait_ge(wo_ld, 16 * KT)
                        copy(wo_hi[:, kt, :], wo_in[:, kt, :]).then_inc(wo_hi_ready, 1)
                    if age and k == WQ_STEP:
                        act.wait_ge(wq_ld, 16 * KT)
                        wq_high(b - 1)

            stage2_batch(0, 0)
            stage2_batch(1, 1)
            with act.Fori(2, BATCH) as b:
                stage2_batch(b, 2)
            for k in range(SUB - LAG, SUB):
                probs_out(BATCH - 1, k)
            for pair in (2, 3):
                att_high(BATCH - 1, pair)
            wq_high(KT - 1)

            act.wait_ge(b_ld, 32)
            copy(b_hl[:, :, :, 0], b_raw[:, :, :]).then_inc(bhi_ready, 1)

            def wk_high(m, slot, uses):
                act.wait_ge(wk_ld[slot], 16 * uses)
                copy(wk_hi[:, slot, :, :], wk_in[:, slot, :, :]).then_inc(wk_hi_ready, 1)

            def m_high(m, slot):
                for half in range(2):
                    act.wait_ge(m_done, 2 * m + half + 1)
                    copy(m_hi[:, bass.ds(m, 1), half * BANK:(half + 1) * BANK],
                         bank[2 * slot + half][:, :].unsqueeze(1)).then_inc(m_hi_ready, 1)
            wk_high(0, 0, 1)
            wk_high(1, 1, 1)
            act.wait_ge(b_spread, 1)
            copy(cD[:, :], OBANK[:, 0:1]).then_inc(cD_ready, 1)
            with act.Fori(0, KT // 2 - 1) as m2:
                m_high(2 * m2, 0)
                wk_high(2 * m2 + 2, 0, m2 + 2)
                m_high(2 * m2 + 1, 1)
                wk_high(2 * m2 + 3, 1, m2 + 2)
            m_high(KT - 2, 0)
            m_high(KT - 1, 1)
            for half in range(2):
                act.wait_ge(b_spread, half + 3)
                copy(u_bc[:, half * BANK:(half + 1) * BANK], WBANK[half][:, :]).then_inc(ubc_ready, 1)

            def ctx_high(g, kt):
                act.wait_ge(cps_ready, KT * g + kt + 1)
                copy(cT_hi[:, kt, :], CPS[kt % 2][:, :]).then_inc(cT_hi_ready, 1)

            def key_high(g, a, it):
                act.wait_ge(acc_done, use_of(g, key_use(it)) + 1)
                nc.scalar.activation(k_hi[:, it, :], acc_bank(a, key_use(it))[:, :], ACT.Identity, bias=bA[:, it:it + 1])\
                    .then_inc(k_hi_ready, 1)

            def x1_high(g, t):
                if t:
                    act.wait_ge(s2_main, GT * g + t)
                tile_high(X1PS, x1T_hi, 2 * (GT * g + t), x1ps_ready, x1T_hi_ready)

            def exponent2(g, t):
                act.wait_ge(nmax2_ready, GT * g + t + 1)
                nc.scalar.activation(pc[:, t % 2, :], SPS[t % 2][:, 0:SEQ], ACT.Exp, bias=nm2[:, t, 1:2],
                                     scale=CROSS_SCALE, accum_out=rs2[:, t:t + 1]).then_inc(exp2_done, 1)

            def probs_out2(g, t):
                act.wait_ge(p2T_done, GT * g + t + 1)
                copy(pcT[:, t % 2, :, :].rearrange("p i s -> p (i s)"), SPS[t % 2][:, SEQ:2 * SEQ]).then_inc(p2T_ready, 1)

            def x2_high(n, slot):
                tile_high(X2PS, x2T_hi[:, slot, :, :], 2 * n, x2ps_ready, x2T_hi_ready)

            def cross_group(g, a, last):
                def ahead(kt):
                    if not last:
                        ctx_high(g + 1, kt)

                for it in range(1, KT):
                    key_high(g, a, it)
                    if it == 5:
                        x1_high(g, 0)
                x1_high(g, 1)
                ahead(0)
                exponent2(g, 0)
                probs_out2(g, 0)
                x1_high(g, 2)
                exponent2(g, 1)
                ahead(1)
                probs_out2(g, 1)
                ahead(2)
                exponent2(g, 2)
                x1_high(g, 3)
                ahead(3)
                probs_out2(g, 2)
                ahead(4)
                exponent2(g, 3)
                ahead(5)
                ahead(6)
                ahead(7)
                if last:
                    x2_high(0, 0)
                if not last:
                    key_high(g, a, 0)
                probs_out2(g, 3)

            for kt in range(KT):
                ctx_high(0, kt)
            act.wait_ge(bA_ready, 3)
            act.wait_ge(acc_done, 1)
            nc.scalar.activation(k_hi[:, 0, :], ACC[0][:, :], ACT.Identity, bias=bA[:, 0:1]).then_inc(k_hi_ready, 1)
            with act.Fori(0, GROUPS // 2 - 1) as g2:
                cross_group(2 * g2, 0, False)
                cross_group(2 * g2 + 1, 1, False)
            cross_group(GROUPS - 2, 0, False)
            cross_group(GROUPS - 1, 1, True)

            x2_high(1, 1)
            with act.Fori(1, BATCH) as b:
                x2_high(2 * b, 0)
                x2_high(2 * b + 1, 1)

        @block.vector
        def _(dve):
            def low(o, i, hi):
                return nc.vector.tensor_tensor(o, i, hi.bitcast(F32), ALU.subtract)

            def tile_low(banks, dst_hi, dst_lo, first, hi_ready, done):
                flat = lambda w, h: w[:, 4 * h:4 * h + 4, :].rearrange("p k s -> p (k s)")
                for h in range(2):
                    dve.wait_ge(hi_ready, first + h + 1)
                    mm = low(flat(dst_lo, h), banks[h][:, :], flat(dst_hi, h))
                mm.then_inc(done, 1)

            def x_low(n, slot):
                tile_low(XPS, xT_hi[:, slot, :, :], xT_lo[:, slot, :, :], 2 * n, xT_hi_ready, xT_lo_ready)

            def q_low(n, g):
                lo, hi = QBLK[g]
                dve.wait_ge(qT_hi_ready, 3 * n + g + 1)
                if g == 0:
                    wait(dve, qlo_st, 16 * n)
                flat = lambda w: w[:, lo:hi, :].rearrange("p c s -> p (c s)")
                low(flat(qT_lo), QPS[g][:, 0:(hi - lo) * P], flat(qT_hi)).then_inc(qT_lo_ready, 1)

            def f_low(b, banks=XPS):
                for h in range(2):
                    dve.wait_ge(f_hi_ready, 2 * b + h + 1)
                    cols = slice(h * BANK, (h + 1) * BANK)
                    low(f_out[1][:, cols], banks[h][:, :], f_out[0][:, cols]).then_inc(f_lo_ready, 1)

            def sines(n, j, c):
                dve.wait_ge(raw_ready[c], n + 1)
                wait(dve, turned_ready[c], n)
                for lo, hi, ty in PIECE[c]:
                    pair = lambda w, i: w[:, lo:hi].rearrange("p (h d i) -> p h d i", i=2, d=HD // 2)[:, :, :, i]
                    nh = (hi - lo) // HD
                    for i, at in ((0, HD), (1, HD + HD // 2)):
                        sn = tab[:, j, ty, at:at + HD // 2].unsqueeze(1).to_broadcast([P, nh, HD // 2])
                        mm = nc.vector.tensor_tensor(pair(rot_s, i), pair(raw, 1 - i), sn, ALU.mult)
                mm.then_inc(sin_done[c], 1)

            A, B, C, T = pick

            def decode(b):
                def spread(s0, s1):
                    def go():
                        if s0 == 0:
                            wait(dve, pick_step, PICKS * b)
                            dve.wait_ge(planes_ld, 16 * b + 16)
                        for s in range(s0, s1):
                            mm = nc.vector.tensor_scalar(bits[:, :, :].rearrange("p q (w s) -> p q w s", s=32)[:, :, :, s],
                                                         planes[:, :, :], 31 - s, 31, ALU.logical_shift_left,
                                                         ALU.arith_shift_right)
                        if s1 == 32:
                            mm.then_inc(bits_ready, 1)
                            dve.wait_ge(lut_ld, 16 * b + 16)
                            nc.vector.tensor_tensor(lut_x[:, :], lut[:, 0:LEVELS:2].bitcast(I32),
                                                    lut[:, 1:LEVELS:2].bitcast(I32), ALU.bitwise_xor).then_inc(lutx_ready, 1)
                    return go

                count = [0]

                def leaf(o, i, after=0):
                    at = count[0]
                    count[0] += 1

                    def go():
                        if at == 0:
                            dve.wait_ge(bits_ready, b + 1)
                            dve.wait_ge(lutx_ready, b + 1)
                            wait(dve, fps_ready, 2 * b)
                        if o is C:
                            wait(dve, f_stored, 32 * b)
                        if after:
                            dve.wait_ge(pick_step, PICKS * b + after)
                        nc.vector.tensor_scalar(o[:, :], bits[:, 0, :], lut_x[:, i:i + 1],
                                                lut[:, 2 * i:2 * i + 1].bitcast(I32), ALU.bitwise_and, ALU.bitwise_xor)\
                            .then_inc(pick_step, 1)
                    return go

                def choose(o, bit, other):
                    at = count[0]
                    count[0] += 1

                    def go():
                        wait_alone(dve, pick_step, PICKS * b + at)
                        nc.vector.copy_predicated(o[:, :], bits[:, bit, :], other[:, :]).then_inc(pick_step, 1)
                    return go

                tree = [leaf(A, 0), leaf(B, 1), choose(A, 1, B), leaf(B, 2, 3), leaf(C, 3), choose(B, 1, C), choose(A, 2, B),
                        leaf(B, 4, 7), leaf(C, 5), choose(B, 1, C), leaf(C, 6, 10), leaf(T, 7), choose(C, 1, T), choose(B, 2, C),
                        choose(A, 3, B)]
                return [[spread(0, 18)], [spread(18, 32)], tree[0:4], tree[4:8], tree[8:12], tree[12:15]]

            def stage1_batch(b, first, last):
                parts = decode(b)
                for j in range(2):
                    n = 2 * b + j
                    for c in range(3):
                        sines(n, j, c)
                        if not (first and j == 0):
                            if c == 0:
                                for g in range(3) if first else (2,):
                                    q_low(n - 1, g)
                                if j == 0:
                                    f_low(b - 1)
                            elif c == 1:
                                q_low(n, 0)
                                if not (last and j == 1):
                                    x_low(n + 1, 1 - j)
                            else:
                                q_low(n, 1)
                        if last and j == 1 and c == 2:
                            return parts[-1]
                        for go in parts[3 * j + c]:
                            go()

            x_low(0, 0)
            for kt in range(KT):
                dve.wait_ge(w_hi_ready, kt + 1)
                low(w_lo[:, kt, :], w_in[:, kt, :], w_hi[:, kt, :]).then_inc(w_lo_ready, 1)
            x_low(1, 1)
            dve.wait_ge(tab_ld, 16)
            stage1_batch(0, True, False)
            with dve.Fori(1, BATCH - 1) as b:
                stage1_batch(b, False, False)
            last_picks = stage1_batch(BATCH - 1, False, True)

            def maxima(b, k):
                u, pos = SUB * b + k, k % 3
                dve.wait_ge(s_done, u + 1)
                wait(dve, exp_done, u - 3)
                n, keys = len(heads_of(pos)), keys_of(pos)
                nc.vector.tensor_reduce(nmax[:, k % 4, 0:n], SBANK[pos][:, :].rearrange("p (h t) -> p h t", t=keys),
                                        axis=AX.X, op=ALU.max, negate=True).then_inc(nmax_ready, 1)

            def inverse(b, k):
                u, n = SUB * b + k, len(heads_of(k % 3))
                dve.wait_ge(exp_done, u + 1)
                wait(dve, prob_ready, u - 3)
                nc.vector.reciprocal(rinv[:, k % 4, 0:n], rsum[:, k % 4, 0:n]).then_inc(rinv_ready, 1)

            def probs_out(b, k):
                u, pos = SUB * b + k, k % 3
                if pos == 1:
                    dve.wait_ge(pT_done, u + 1)
                    wait(dve, pv_done, probT_used(b, k))
                    nc.vector.tensor_copy(probT[:, k % 4, :], TBANK[k % 2][:, :]).then_inc(pT_dve, 1)

            def out_unit(b, k, behind):
                unit = k // 3
                if k % 3 == 2:
                    dve.wait_ge(pv_done, 2 * (KVH * b + unit + 1))
                    if behind:
                        dve.wait_ge(att_hi_ready, 4 * (b - 1) + unit // 2 + 1)
                    nc.vector.tensor_copy(att[:, unit, :], OBANK[:, 0:SEQ]).then_inc(att_ready, 1)

            def att_low(b, pair):
                dve.wait_ge(att_hi_ready, 4 * b + pair + 1)
                flat = lambda w: w[:, 2 * pair:2 * pair + 2, :].rearrange("p k s -> p (k s)")
                low(flat(att_lo), flat(att), flat(att_hi)).then_inc(att_lo_ready, 1)

            def add_part(b, g):
                st, half = g // 2, g % 2
                cols = slice(half * BANK, (half + 1) * BANK)
                dve.wait_ge(wo_done, 4 * b + g + 1)
                if half == 0:
                    dve.wait_ge(y1_ld[st], 16 * b + 16)
                nc.vector.tensor_tensor(y1[:, st, cols], WBANK[g % 2][:, :], y1[:, st, cols], ALU.add).then_inc(y1_part, 1)
                dve.wait_ge(y1_part, 4 * b + g + 1)
                nc.vector.bn_stats(st1[:, st, half, :], y1[:, st, cols]).then_inc(y1_stats, 1)
                if half == 1:
                    wait_alone(dve, y1_stats, 4 * b + g + 1)
                    nc.vector.bn_aggr(mv1[:, st, :], st1[:, st, :, :].rearrange("p h s -> p (h s)")).then_inc(y1_mv, 1)
                    dve.wait_ge(y1_mv, 2 * b + st + 1)
                    nc.vector.tensor_scalar_add(rs1[:, st, 0:1], mv1[:, st, 1:2], EPS).then_inc(y1_var, 1)

            def normalise(b, st):
                dve.wait_ge(y1_rstd, 2 * b + st + 1)
                nc.vector.tensor_scalar(y1[:, st, :], y1[:, st, :], mv1[:, st, 0:1], rs1[:, st, 1:2], ALU.subtract,
                                        ALU.mult).then_inc(y1_ready, 1)

            def late(b, k, what, *more):
                what(b - 1, k + SUB, *more) if k < 0 else what(b, k, *more)

            def wq_low(dt):
                one = lambda w: w[:, bass.ds(dt, 1), :]
                dve.wait_ge(wq_hi_ready, dt + 1)
                low(one(wq_lo), one(wq_in), one(wq_hi)).then_inc(wq_lo_ready, 1)

            def stage2_batch(b, age):
                for k in range(SUB):
                    maxima(b, k)
                    if age or k >= 1:
                        late(b, k - 1, inverse)
                    if k in ADD_STEP and ADD_STEP[k][0] <= age:
                        add_part(b - ADD_STEP[k][0], ADD_STEP[k][1])
                    if age or k >= LAG:
                        late(b, k - LAG, probs_out)
                    if k >= OUT_LAG:
                        out_unit(b, k - OUT_LAG, age > 0)
                    elif age:
                        out_unit(b - 1, k - OUT_LAG + SUB, False)
                    if k in LOW_STEP and LOW_STEP[k][0] <= age:
                        att_low(b - LOW_STEP[k][0], LOW_STEP[k][1])
                    if age == 0 and k == Q_TAIL_STEP:
                        q_low(TILES - 1, 2)
                        for j in range(2):
                            dve.wait_ge(v_stored[j], 16 * BATCH)
                    if age == 0 and 3 <= k < 3 + len(last_picks):
                        last_picks[k - 3]()
                    if age == 0 and k == F_TAIL_STEP:
                        f_low(BATCH - 1, WBANK)
                    if age == 0 and k - 1 in WO_STEPS:
                        kt = WO_STEPS[k - 1]
                        dve.wait_ge(wo_hi_ready, kt + 1)
                        low(wo_lo[:, kt, :], wo_in[:, kt, :], wo_hi[:, kt, :]).then_inc(wo_lo_ready, 1)
                    if age and k == WQ_STEP:
                        wq_low(b - 1)
                    if k in NORM_STEP and NORM_STEP[k][0] <= age:
                        normalise(b - NORM_STEP[k][0], NORM_STEP[k][1])

            stage2_batch(0, 0)
            stage2_batch(1, 1)
            with dve.Fori(2, BATCH) as b:
                stage2_batch(b, 2)
            inverse(BATCH - 1, SUB - 1)
            for k in range(SUB, SUB + OUT_LAG):
                if k - LAG < SUB:
                    probs_out(BATCH - 1, k - LAG)
                out_unit(BATCH - 1, k - OUT_LAG, True)
            for pair in (1, 2, 3):
                att_low(BATCH - 1, pair)
            add_part(BATCH - 2, 3)
            normalise(BATCH - 2, 1)
            wq_low(KT - 1)

            dve.wait_ge(b_ld, 32)
            nc.vector.tensor_tensor(b_prod[:, :], b_raw[:, 0, :], b_raw[:, 1, :], ALU.mult).then_inc(b_part_step, 1)
            dve.wait_ge(bhi_ready, 1)
            low(b_hl[:, :, :, 1], b_raw[:, :, :], b_hl[:, :, :, 0]).then_inc(blo_ready, 1)
            dve.wait_ge(b_part_step, 1)
            nc.vector.tensor_reduce(b_part[:, :], b_prod[:, :], axis=AX.X, op=ALU.add).then_inc(b_part_step, 1)

            def wk_low(m, slot):
                dve.wait_ge(wk_hi_ready, m + 1)
                low(wk_lo[:, slot, :, :], wk_in[:, slot, :, :], wk_hi[:, slot, :, :]).then_inc(wk_lo_ready, 1)

            def u_row(m):
                dve.wait_ge(u_done, m + 1)
                nc.vector.tensor_copy(b_rows[0:2, 0, bass.ds(m * P, P)], bank[6][0:2, 0:P]).then_inc(urow_ready, 1)

            def m_low(m, slot):
                for half in range(2):
                    dve.wait_ge(m_hi_ready, 2 * m + half + 1)
                    row = lambda w: w[:, bass.ds(m, 1), half * BANK:(half + 1) * BANK]
                    low(row(m_lo), bank[2 * slot + half][:, :].unsqueeze(1), row(m_hi)).then_inc(m_lo_ready, 1)

            wk_low(0, 0)
            wk_low(1, 1)
            for g in range(4):
                add_part(BATCH - 1, g)
                if g % 2:
                    normalise(BATCH - 1, g // 2)
            m_low(0, 0)
            u_row(0)
            for half, o in enumerate((bank[7], bank[4])):
                dve.wait_ge(bA_done, half + 1)
                nc.vector.tensor_copy(b_rows[0:2, 1, half * BANK:(half + 1) * BANK], o[0:2, :]).then_inc(bA_ready, 1)
            u_row(1)
            wk_low(2, 0)
            m_low(1, 1)
            wk_low(3, 1)
            with dve.Fori(1, KT // 2 - 1) as m2:
                for slot in range(2):
                    u_row(2 * m2 + slot)
                    m_low(2 * m2 + slot, slot)
                    wk_low(2 * m2 + slot + 2, slot)
            for slot in range(2):
                u_row(KT - 2 + slot)
                m_low(KT - 2 + slot, slot)
            dve.wait_ge(b_spread, 2)
            nc.vector.tensor_copy(bA[:, :], OBANK[:, 0:KT]).then_inc(bA_ready, 1)

            def ctx_low(g, kt):
                dve.wait_ge(cT_hi_ready, KT * g + kt + 1)
                low(cT_lo[:, kt, :], CPS[kt % 2][:, :], cT_hi[:, kt, :]).then_inc(cps_free, 1)

            def block_low(o, sums, bias_col, hi):
                return nc.vector.scalar_tensor_tensor(out=o, in0=sums, scalar=bias_col, in1=hi.bitcast(F32), op0=ALU.add,
                                                      op1=ALU.subtract)

            def key_low(g, a, it):
                dve.wait_ge(k_hi_ready, KT * g + (it if it else KT) + 1)
                block_low(k_lo[:, it, :], acc_bank(a, key_use(it))[:, :], bA[:, it:it + 1], k_hi[:, it, :]).then_inc(acc_free, 1)

            def key_sum(g, t):
                dve.wait_ge(cu_ready, GT * g + t + 1)
                nc.vector.tensor_reduce(s_sum[:, t:t + 1], cu[:, :], axis=AX.X, op=ALU.add).then_inc(cu_free, 1)

            def key_diagonals(g):
                dve.wait_ge(cu_free, GT * g + GT + 1)
                nc.vector.tensor_scalar_add(s_key[:, :], s_sum[:, :], cD[:, 0:1]).then_inc(s_ready, 1)
                dve.wait_ge(s_ready, g + 1)
                for t in range(GT):
                    nc.vector.tensor_scalar_mul(d_hi[:, t * P:(t + 1) * P], ident[:, :], s_key[:, t:t + 1]).then_inc(d_hi_ready, 1)
                for t in range(GT):
                    dve.wait_ge(d_hi_ready, GT * g + t + 1)
                    nc.vector.scalar_tensor_tensor(out=d_lo[:, t * P:(t + 1) * P], in0=ident[:, :], scalar=s_key[:, t:t + 1],
                                                   in1=d_hi[:, t * P:(t + 1) * P].bitcast(F32), op0=ALU.mult, op1=ALU.subtract)\
                        .then_inc(d_ready, 1)

            def x1_low(g, t):
                flat = lambda w, h: w[:, 4 * h:4 * h + 4, :].rearrange("p k s -> p (k s)")
                for h in range(2):
                    dve.wait_ge(x1T_hi_ready, 2 * (GT * g + t) + h + 1)
                    low(flat(x1T_lo, h), X1PS[h][:, :], flat(x1T_hi, h)).then_inc(x1ps_free, 1)

            def maxima2(g, t):
                dve.wait_ge(s2_done, GT * g + t + 1)
                nc.vector.tensor_reduce(nm2[:, t, 0:1], SPS[t % 2][:, 0:SEQ], axis=AX.X, op=ALU.max, negate=True)\
                    .then_inc(nmax2_raw, 1)
                dve.wait_ge(nmax2_raw, GT * g + t + 1)
                nc.vector.tensor_scalar_mul(nm2[:, t, 1:2], nm2[:, t, 0:1], CROSS_SCALE).then_inc(nmax2_ready, 1)

            def add_cross(g, a, t, last):
                dve.wait_ge(exp2_done, GT * g + t + 1)
                nc.vector.reciprocal(ri2[:, t:t + 1], rs2[:, t:t + 1]).then_inc(rinv2_ready, 1)
                dve.wait_ge(rinv2_ready, GT * g + t + 1)
                for half in range(2):
                    i, cols = att_use(t, half, last), slice(half * BANK, (half + 1) * BANK)
                    dve.wait_ge(acc_done, use_of(g, i) + 1)
                    nc.vector.scalar_tensor_tensor(out=x1_st[:, t, cols], in0=acc_bank(a, i)[:, :], scalar=ri2[:, t:t + 1],
                                                   in1=x1_st[:, t, cols], op0=ALU.mult, op1=ALU.add).then_inc(acc_free, 1)
                    dve.wait_ge(acc_free, use_of(g, i) + 3)
                    nc.vector.bn_stats(st2[:, t, half, :], x1_st[:, t, cols]).then_inc(y2_stats, 1)
                wait_alone(dve, y2_stats, 2 * (GT * g + t) + 2)
                nc.vector.bn_aggr(mv2[:, t, :], st2[:, t, :, :].rearrange("p h s -> p (h s)")).then_inc(y2_mv, 1)
                dve.wait_ge(y2_mv, GT * g + t + 1)
                nc.vector.tensor_scalar_add(rv2[:, t, 0:1], mv2[:, t, 1:2], EPS).then_inc(y2_var, 1)

            def normalise2(g, t):
                dve.wait_ge(y2_rstd, GT * g + t + 1)
                nc.vector.tensor_scalar(x1_st[:, t, :], x1_st[:, t, :], mv2[:, t, 0:1], rv2[:, t, 1:2], ALU.subtract,
                                        ALU.mult).then_inc(y2_ready, 1)

            def x2_low(n, slot):
                tile_low(X2PS, x2T_hi[:, slot, :, :], x2T_lo[:, slot, :, :], 2 * n, x2T_hi_ready, x2T_lo_ready)

            def cross_group(g, a, last):
                def ahead(kt):
                    if not last:
                        ctx_low(g + 1, kt)

                for it in range(1, KT):
                    key_low(g, a, it)
                    if it <= GT:
                        key_sum(g, it - 1)
                    if it == 5:
                        x1_low(g, 0)
                    if it == 6:
                        key_diagonals(g)
                x1_low(g, 1)
                ahead(0)
                maxima2(g, 0)
                x1_low(g, 2)
                maxima2(g, 1)
                ahead(1)
                add_cross(g, a, 0, last)
                ahead(2)
                normalise2(g, 0)
                maxima2(g, 2)
                x1_low(g, 3)
                ahead(3)
                add_cross(g, a, 1, last)
                ahead(4)
                normalise2(g, 1)
                maxima2(g, 3)
                ahead(5)
                add_cross(g, a, 2, last)
                ahead(6)
                ahead(7)
                normalise2(g, 2)
                if not last:
                    key_low(g, a, 0)
                if last:
                    x2_low(0, 0)
                add_cross(g, a, 3, last)
                normalise2(g, 3)

            dve.wait_ge(cD_ready, 1)
            dve.sem_inc(cps_free, 2)
            dve.sem_inc(x1ps_free, 2)
            dve.sem_inc(cu_free, 1)
            dve.sem_inc(acc_free, 2)
            for kt in range(KT):
                ctx_low(0, kt)
            dve.wait_ge(k_hi_ready, 1)
            block_low(k_lo[:, 0, :], ACC[0][:, :], bA[:, 0:1], k_hi[:, 0, :]).then_inc(acc_free, 1)
            with dve.Fori(0, GROUPS // 2 - 1) as g2:
                cross_group(2 * g2, 0, False)
                cross_group(2 * g2 + 1, 1, False)
            cross_group(GROUPS - 2, 0, False)
            cross_group(GROUPS - 1, 1, True)

            def ffn_batch(b, last):
                for j in range(2):
                    n = 2 * b + j
                    if not (last and j == 1):
                        x2_low(n + 1, 1 - j)
                    dve.wait_ge(x2b_ready, n + 1)
                    wait(dve, out_stored[j], 16 * b)
                    for half in range(2):
                        cols = slice(half * BANK, (half + 1) * BANK)
                        dve.wait_ge(ffn_done, 2 * n + half + 1)
                        nc.vector.tensor_tensor(y3[:, j, cols], YPS[j][half][:, :], x2b[:, j, cols], ALU.add)\
                            .then_inc(y3_part, 1)
                        dve.wait_ge(y3_part, 2 * n + half + 1)
                        nc.vector.bn_stats(st3[:, j, half, :], y3[:, j, cols]).then_inc(y3_stats, 1)
                    wait_alone(dve, y3_stats, 2 * n + 2)
                    nc.vector.bn_aggr(mv3[:, j, :], st3[:, j, :, :].rearrange("p h s -> p (h s)")).then_inc(y3_mv, 1)
                    dve.wait_ge(y3_mv, n + 1)
                    nc.vector.tensor_scalar_add(rv3[:, j, 0:1], mv3[:, j, 1:2], EPS).then_inc(y3_var, 1)
                    dve.wait_ge(y3_rstd, n + 1)
                    nc.vector.tensor_scalar(y3[:, j, :], y3[:, j, :], mv3[:, j, 0:1], rv3[:, j, 1:2], ALU.subtract,
                                            ALU.mult).then_inc(y3_ready, 1)
            ffn_batch(0, False)
            with dve.Fori(1, BATCH - 1) as b:
                ffn_batch(b, False)
            ffn_batch(BATCH - 1, True)

        @block.gpsimd
        def _(pool):
            nc.gpsimd.memset(ident[:, :], 0.0)
            nc.gpsimd.memset(rot_c[:, 0:BANK], 0.0)
            nc.gpsimd.memset(ones[:, :], 1.0)
            nc.gpsimd.memset(neg_half[:, :], -0.5).then_inc(consts_step, 1)
            pool.wait_ge(consts_step, 1)
            nc.gpsimd.affine_select(out=ident[:, :], in_=ident[:, :], compare_op=ALU.not_equal, fill=1.0, base=0,
                                    pattern=[[-1, P]], channel_multiplier=1).then_inc(consts_step, 1)
            m3 = rot_c[:, 0:BANK].rearrange("p (h t) -> p h t", t=P)
            nc.gpsimd.affine_select(out=m3, in_=m3, compare_op=ALU.is_ge, fill=MASKED, base=0,
                                    pattern=[[0, REP], [-1, P]], channel_multiplier=1).then_inc(consts_step, 1)
            pool.wait_ge(consts_step, 3)
            nc.gpsimd.tensor_copy(ident_r[:, :], ident[:, :])
            nc.gpsimd.tensor_copy(mask_r[:, :, :].rearrange("p h t -> p (h t)"), rot_c[:, 0:BANK])
            nc.gpsimd.tensor_copy(ones_r[:, :], ones[:, :]).then_inc(consts_done, 1)

            def cosines(n, j, c):
                pool.wait_ge(raw_ready[c], n + 1)
                for lo, hi, ty in PIECE[c]:
                    nh = (hi - lo) // HD
                    head = lambda w: w[:, lo:hi].rearrange("p (h d) -> p h d", d=HD)
                    cs = tab[:, j, ty, 0:HD].unsqueeze(1).to_broadcast([P, nh, HD])
                    mm = nc.gpsimd.tensor_tensor(head(rot_c), head(raw), cs, ALU.mult)
                mm.then_inc(cos_done[c], 1)

            def turned_chunk(n, c):
                lo, hi = c * BANK, min((c + 1) * BANK, ROPE)
                pool.wait_ge(cos_done[c], n + 1)
                pool.wait_ge(sin_done[c], n + 1)
                wait(pool, qps_ready[c], n)
                nc.gpsimd.tensor_tensor(turned[:, lo:hi], rot_c[:, lo:hi], rot_s[:, lo:hi], ALU.add)\
                    .then_inc(turned_ready[c], 1)

            pool.wait_ge(tab_ld, 16)
            pool.wait_ge(consts_done, 1)

            def stage1_batch(b):
                for j in range(2):
                    for c in range(3):
                        cosines(2 * b + j, j, c)
                        turned_chunk(2 * b + j, c)

            stage1_batch(0)
            with pool.Fori(1, BATCH) as b:
                stage1_batch(b)

            def rstd1(b, st):
                pool.wait_ge(y1_var, 2 * b + st + 1)
                nc.gpsimd.tensor_tensor(rs1[:, st, 1:2], rs1[:, st, 0:1], neg_half[:, :], ALU.pow).then_inc(y1_rstd, 1)

            def scale_probs(b, k):
                u, pos = SUB * b + k, k % 3
                n, keys = len(heads_of(pos)), keys_of(pos)
                pool.wait_ge(rinv_ready, u + 1)
                pr = prob[:, k % 4, :].rearrange("p (h t) -> p h t", t=keys)
                nc.gpsimd.tensor_tensor(pr, pr, rinv[:, k % 4, 0:n].unsqueeze(2).to_broadcast([P, n, keys]), ALU.mult)\
                    .then_inc(prob_ready, 1)

            def stage2_batch(b, age):
                for k in range(SUB):
                    if k in RSTD_STEP and RSTD_STEP[k][0] <= age:
                        rstd1(b - RSTD_STEP[k][0], RSTD_STEP[k][1])
                    scale_probs(b, k)

            stage2_batch(0, 0)
            stage2_batch(1, 1)
            with pool.Fori(2, BATCH) as b:
                stage2_batch(b, 2)
            rstd1(BATCH - 2, 1)
            for st in range(2):
                rstd1(BATCH - 1, st)

            def context_by_u(g, a):
                pool.wait_ge(ctx_ld[a], GT * 8 * (g - a + 2))
                for t in range(GT):
                    pool.wait_ge(cu_free, GT * g + t + 1)
                    nc.gpsimd.tensor_tensor(cu[:, :], ctx_st[:, a, t, :], u_bc[:, :], ALU.mult).then_inc(cu_ready, 1)

            pool.wait_ge(ubc_ready, 2)
            with pool.Fori(0, GROUPS // 2) as g2:
                for a in range(2):
                    g = 2 * g2 + a
                    context_by_u(g, a)
                    for t in range(GT):
                        pool.wait_ge(y2_var, GT * g + t + 1)
                        nc.gpsimd.tensor_tensor(rv2[:, t, 1:2], rv2[:, t, 0:1], neg_half[:, :], ALU.pow).then_inc(y2_rstd, 1)

            pool.wait_ge(bias_ld, 16)
            with pool.Fori(0, BATCH) as b:
                for j in range(2):
                    n = 2 * b + j
                    pool.wait_ge(x2_ld[j], 16 * b + 16)
                    nc.gpsimd.tensor_tensor(x2b[:, j, :], x2_st[:, j, :], bias_bc[:, :], ALU.add).then_inc(x2b_ready, 1)
                    pool.wait_ge(y3_var, n + 1)
                    nc.gpsimd.tensor_tensor(rv3[:, j, 1:2], rv3[:, j, 0:1], neg_half[:, :], ALU.pow).then_inc(y3_rstd, 1)


def kernel(x, ctx_4096, L0_attn_w_qkv, L0_attn_w_o, L0_xattn_Wq, L0_xattn_bq, L0_xattn_Wk, L0_xattn_bk, L0_ffn_qweight,
           L0_ffn_lut4, L0_ffn_lut8, L0_ffn_bias):
    import concourse.bacc as bacc
    from concourse.bass_utils import run_bass_kernel_spmd

    arrays = {"x": x, "ctx_in": ctx_4096, "w_qkv": L0_attn_w_qkv, "w_o": L0_attn_w_o, "wq": L0_xattn_Wq,
              "bq": L0_xattn_bq, "wk": L0_xattn_Wk, "bk": L0_xattn_bk, "qweight": L0_ffn_qweight, "lut4": L0_ffn_lut4,
              "bias": L0_ffn_bias, "rope": rope_tables()}
    arrays = {name: np.ascontiguousarray(a) for name, a in arrays.items()}
    nc = bacc.Bacc("TRN2", target_bir_lowering=False, num_devices=1)
    aps = {name: nc.dram_tensor(name, a.shape, mybir.dt.from_np(a.dtype), kind="ExternalInput").ap()
           for name, a in arrays.items()}
    out = nc.dram_tensor("out", (BATCH, SEQ, D), F32, kind="ExternalOutput").ap()
    decoder_layer(nc, out=out, **aps)
    r = run_bass_kernel_spmd(nc, [arrays], core_ids=[0])
    return r.results[0]["out"]
```
